# Optimizing a Trainium2 kernel written in Bass

```python
import numpy as np
import jax
import jax.numpy as jnp

def _softmax(x, axis=-1):
    return jax.nn.softmax(x, axis=axis)

def _gelu(x):
    return jax.nn.gelu(x, approximate=True)

def _silu(x):
    return jax.nn.silu(x)

def _sigmoid(x):
    return jax.nn.sigmoid(x)

def _layernorm(x, axis=-1, eps=1e-05):
    m = jnp.mean(x, axis=axis, keepdims=True)
    v = jnp.var(x, axis=axis, keepdims=True)
    return (x - m) / jnp.sqrt(v + eps)

def _scatter_add(tgt, idx, src, axis=0):
    return tgt.at[idx].add(src)

def _segment_sum(src, seg, n):
    return jax.ops.segment_sum(src, seg, n)
kernel_name = 'mk_macaron_d1_jaxref_r4_a1d12e'

def setup_inputs(seed: int=0):
    np.random.seed(seed)
    _w = jnp.asarray

    def _L0_attn_setup():
        import jax, jax.numpy as jnp
        import numpy as np
        D_MODEL = 512
        key = jax.random.key(seed)
        kx, kw, kb = jax.random.split(key, 3)
        B, T, D = (4, 1024, D_MODEL)
        x = jax.random.normal(kx, (B, T, D), dtype=jnp.float32)
        scale = 1.0 / np.sqrt(D)
        W = jax.random.uniform(kw, (D, 3 * D), dtype=jnp.float32, minval=-scale, maxval=scale)
        b = jax.random.uniform(kb, (3 * D,), dtype=jnp.float32, minval=-scale, maxval=scale)
        return {'x': x, 'W': W, 'b': b}
    _L0_attn_in = _L0_attn_setup()

    def _L0_ffn_setup():
        import jax, jax.numpy as jnp
        import numpy as np
        EPS = 1e-06
        Q_B = 128.0

        def layer_norm(x):
            mean = jnp.mean(x, axis=-1, keepdims=True)
            var = jnp.var(x, axis=-1, keepdims=True)
            return (x - mean) / jnp.sqrt(var + EPS)

        def absmax_quant(x):
            gamma = jnp.max(jnp.abs(x), axis=-1, keepdims=True)
            x_hat = jnp.clip(x * Q_B / gamma, -Q_B + EPS, Q_B - EPS)
            return x_hat * gamma / Q_B

        def ternarize_weights(w):
            gamma = jnp.mean(jnp.abs(w))
            return jnp.sign(jnp.round(w / (gamma + EPS))) * gamma

        def bitlinear(x, w):
            xn = layer_norm(x)
            x_hat = xn + jax.lax.stop_gradient(absmax_quant(xn) - xn)
            w_hat = w + jax.lax.stop_gradient(ternarize_weights(w) - w)
            return jnp.einsum('bsd,od->bso', x_hat, w_hat)
        key = jax.random.key(seed)
        k1, k2, k3 = jax.random.split(key, 3)
        B, S, D = (4, 512, 512)
        x = jax.random.normal(k1, (B, S, D), dtype=jnp.float32)
        w_fc = jax.random.normal(k2, (4 * D, D), dtype=jnp.float32) / np.sqrt(D)
        w_proj = jax.random.normal(k3, (D, 4 * D), dtype=jnp.float32) / np.sqrt(4 * D)
        return {'x': x, 'w_fc': w_fc, 'w_proj': w_proj}
    _L0_ffn_in = _L0_ffn_setup()
    _d = {'L0_attn_x': _L0_attn_in['x'], 'L0_attn_W': _L0_attn_in['W'], 'L0_attn_b': _L0_attn_in['b'], 'L0_ffn_w_fc': _L0_ffn_in['w_fc'], 'L0_ffn_w_proj': _L0_ffn_in['w_proj']}
    _x0 = _d['L0_attn_x']
    _d['L0_attn_x'] = jax.random.normal(jax.random.fold_in(jax.random.key(seed), 1), (2, 2048, 512), dtype=_x0.dtype)
    del _x0
    return _d

def reference(L0_attn_x, L0_attn_W, L0_attn_b, L0_ffn_w_fc, L0_ffn_w_proj):

    def _L0_attn_ref(x, W, b):
        import jax, jax.numpy as jnp
        import numpy as np
        D_MODEL = 512
        qkv = x @ W + b
        q, k, v = jnp.split(qkv, 3, axis=-1)
        qn = q / jnp.linalg.norm(q, axis=1, keepdims=True)
        kn = k / jnp.linalg.norm(k, axis=1, keepdims=True)
        kv = jnp.sum(kn * v, axis=1, keepdims=True)
        return qn * kv

    def _L0_ffn_ref(x, w_fc, w_proj):
        import jax, jax.numpy as jnp
        import numpy as np
        EPS = 1e-06
        Q_B = 128.0

        def layer_norm(x):
            mean = jnp.mean(x, axis=-1, keepdims=True)
            var = jnp.var(x, axis=-1, keepdims=True)
            return (x - mean) / jnp.sqrt(var + EPS)

        def absmax_quant(x):
            gamma = jnp.max(jnp.abs(x), axis=-1, keepdims=True)
            x_hat = jnp.clip(x * Q_B / gamma, -Q_B + EPS, Q_B - EPS)
            return x_hat * gamma / Q_B

        def ternarize_weights(w):
            gamma = jnp.mean(jnp.abs(w))
            return jnp.sign(jnp.round(w / (gamma + EPS))) * gamma

        def bitlinear(x, w):
            xn = layer_norm(x)
            x_hat = xn + jax.lax.stop_gradient(absmax_quant(xn) - xn)
            w_hat = w + jax.lax.stop_gradient(ternarize_weights(w) - w)
            return jnp.einsum('bsd,od->bso', x_hat, w_hat)
        h = bitlinear(x, w_fc)
        h = jax.nn.gelu(h, approximate=False)
        return bitlinear(h, w_proj)
    x = L0_attn_x
    x = x + 0.5 * _L0_ffn_ref(_layernorm(x, axis=-1), L0_ffn_w_fc, L0_ffn_w_proj)
    x = x + _L0_attn_ref(_layernorm(x, axis=-1), L0_attn_W, L0_attn_b)
    x = x + 0.5 * _L0_ffn_ref(_layernorm(x, axis=-1), L0_ffn_w_fc, L0_ffn_w_proj)
    return x

_drawn_inputs = setup_inputs


def setup_inputs(seed=0):
    import zlib

    import numpy as np

    out = dict(_drawn_inputs(seed))
    spreads = {}
    factors = {'L0_attn_b': 8.0}
    for name, (base, spread) in spreads.items():
        noise = np.random.default_rng([zlib.crc32(name.encode()), seed]).standard_normal(out[name].shape)
        drawn = base * np.exp(spread * noise) if base else spread * noise
        out[name] = jnp.asarray(drawn.astype(out[name].dtype))
    for name, factor in factors.items():
        out[name] = (out[name] * factor).astype(out[name].dtype)
    return out
```

```python
from contextlib import ExitStack

import concourse.bass as bass
from concourse import mybir

F32 = mybir.dt.float32
F16 = mybir.dt.float16
ALU = mybir.AluOpType
ACT = mybir.ActivationFunctionType
AX = mybir.AxisListType

P = 128
EPS_LN = 1e-5
EPS_BIT = 1e-6
XS = 2048.0
US = 1024.0
GS = 2.0 ** -5
TS = GS * US


def wait(eng, sem, value):
    if isinstance(value, int) and value <= 0:
        return
    eng.wait_ge(sem, value)


def macaron_kernel(nc, x, WT, W, b, wfT, wpT, out):
    NB, T, D = x.shape
    F = wfT.shape[1]
    DC = D // P
    FB = F // P
    SUB = 4
    TOK = SUB * P
    NT = NB * T // TOK
    TPB = T // TOK
    LAG = 4
    STEPS = FB
    NS = NT * SUB

    x_v = x.rearrange("b (s p) d -> p (b s) d", p=P)
    out_v = out.rearrange("b (s p) d -> p (b s) d", p=P)
    wf_v = wfT.rearrange("(c p) f -> p c f", p=P)
    wp_v = wpT.rearrange("(c p) o -> p c o", p=P)
    WT_v = WT.rearrange("(c p) d -> p c d", p=P)
    W_v = W.rearrange("(c p) n -> p c n", p=P)
    b_v = b.rearrange("(c p) -> p c", p=P)

    with ExitStack() as ctx:
        def sb(name, shape, dt=F32):
            return ctx.enter_context(nc.sbuf_tensor(name, shape, dt))

        def sem(name):
            return ctx.enter_context(nc.semaphore(name))

        X = sb("X", [P, NS, D])
        wf = sb("wf", [P, DC, F], F16)
        wp = sb("wp", [P, FB, D], F16)
        xT = sb("xT", [P, 2, DC, TOK], F16)
        qT = sb("qT", [P, 2, 2, DC, P], F16)
        G2 = sb("G2", [P, LAG, 2, TOK], F16)
        U = sb("U", [P, 2, 2, DC, D], F16)
        Gacc = sb("Gacc", [P, DC, D])
        acc1 = sb("acc1", [P, TOK])
        acc2 = sb("acc2", [P, TOK])
        Tsum = sb("Tsum", [P, D])
        Srow = sb("Srow", [P, D])
        Brow = sb("Brow", [P, D])
        bnrow = sb("bnrow", [P, 2, D])
        ones32 = sb("ones32", [P, P])
        ones16 = sb("ones16", [P, P], F16)
        id32 = sb("id32", [P, P])
        id16 = sb("id16", [P, P], F16)
        scratch = sb("scratch", [P, 10240])

        def region(a, n, dt=F32):
            r = scratch[:, a:a + n]
            return r.bitcast(dt) if dt != F32 else r

        hl = region(0, 2048, F16).rearrange("p (h s d) -> p h s d", h=2, s=SUB)
        hlA = region(2048, 2048, F16).rearrange("p (h s d) -> p h s d", h=2, s=SUB)
        hlQ = region(4096, 2048, F16).rearrange("p (h s d) -> p h s d", h=2, s=SUB)
        gf = region(6144, 1024).rearrange("p (r t) -> p r t", r=2)
        sq = region(7168, 1024).rearrange("p (r t) -> p r t", r=2)
        vb = region(8192, 1024).rearrange("p (r t) -> p r t", r=2)
        ub = region(9216, 1024).rearrange("p (r t) -> p r t", r=2)
        sums = region(0, 2048).rearrange("p (r t) -> p r t", r=4)
        sum_mq = region(8192, 512)
        Wst = region(2048, 3072).rearrange("p (r j d) -> p r j d", r=2, j=3)
        GH = region(6144, 2048, F16).rearrange("p (h c d) -> p h c d", h=2, c=DC)
        xk, xq = region(9216, 512), region(8704, 512)
        term = [region(a, 512) for a in (5120, 5632, 9728)]
        wf_st = X[:, 4 * SUB:8 * SUB, :].rearrange("p (c s) d -> p c (s d)", c=DC)
        wp_st = [X[:, 2 * SUB:4 * SUB, :], region(2048, 4096).rearrange("p (c d) -> p c d", d=D)]
        WT_st = X[:, 4 * SUB:6 * SUB, :]
        W_st = X[:, 6 * SUB:8 * SUB, :].rearrange("p (c j) d -> p c j d", c=DC)

        def small(name, *shape):
            return sb(name, [P, *shape])

        st = small("st", SUB, 6)
        stA = small("stA", SUB, 6)
        mF, msum, mdif, vsum, vdif, vtot = (small(n, SUB) for n in ("mF", "msum", "mdif", "vsum", "vdif", "vtot"))
        mA = small("mA", NS)
        ve, pw, rz, zz, rf = (small(n, SUB) for n in ("ve", "pw", "rz", "zz", "rf"))
        veA, pwA = small("veA", SUB), small("pwA", SUB)
        rA = small("rA", NS)
        negm, negmk, m2, var, varc, veP, pwP, rzP, zP, cP = (
            small(n, SUB) for n in ("negm", "negmk", "m2", "var", "varc", "veP", "pwP", "rzP", "zP", "cP"))
        half = small("half", SUB)
        absum = small("absum", 2, 4)
        gam = small("gam", 2)
        theta = small("theta", 2, 2)
        hscale, kap, cs, kinv = (small(n, 1) for n in ("hscale", "kap", "cs", "kinv"))
        mu = small("mu", DC)
        bcol = small("bcol", 12)
        acol, babs, ra, bn, raS = (small(n, 8) for n in ("acol", "babs", "ra", "bn", "raS"))
        red = small("red", 20)
        k1, q1, kk, qq, kv, prod, ip, scol, bsc, sc2 = (
            small(n, DC) for n in ("k1", "q1", "kk", "qq", "kv", "prod", "ip", "scol", "bsc", "sc2"))
        diag = sb("diag", [P, 2, 4, P])

        def bank(name):
            return ctx.enter_context(nc.psum_tensor(name, [P, 512], F32))

        H = [bank("H0"), bank("H1")]
        A = [bank(f"A{s}") for s in range(SUB)]
        S = [bank("S0"), bank("S1")]

        s_x = [sem(f"x_loaded{t}") for t in range(NT)]
        s_wf = [sem(f"wf_loaded{c}") for c in range(DC)]
        s_wp = [sem(f"wp_loaded{c}") for c in range(4)]
        s_WT, s_W, s_b = sem("WT_loaded"), sem("W_loaded"), sem("b_loaded")
        s_wst = [sem("Wchunk_loaded0"), sem("Wchunk_loaded1")]
        out_stored = sem("out_stored")
        const_ready = sem("const_ready")
        abs_dve, abs_act = sem("abs_dve"), sem("abs_act")
        total_ready = sem("total_ready")
        scal = sem("scalars_chain")
        neg_ready = sem("neg_ready")
        tern_f, tern_p = sem("tern_f"), sem("tern_p")
        tsum_ready, tsum_saved = sem("tsum_ready"), sem("tsum_saved")
        ub_chain, ub_diag, ub_row, ub_prod, ub_hi, ub_lo = (
            sem(n) for n in ("u_chain", "u_diag", "u_row", "u_prod", "u_hi", "u_lo"))
        bn_saved = sem("bn_saved")
        ln_stat, ln_aggr, ln_pre, ln_pow, ln_r, ln_v, ln_hi, ln_lo = (
            {k: sem(f"{n}{k}") for k in "FAQ"} for n in
            ("ln_stat", "ln_aggr", "ln_pre", "ln_pow", "ln_r", "ln_v", "ln_hi", "ln_lo"))
        ln_mean = {k: sem(f"ln_mean{k}") for k in "FA"}
        t_ready, t_saved = sem("t_ready"), sem("t_saved")
        h_ready, gelu_done, sq_done, hi_done, lo_done, acc_done, acc_one, proj_done = (
            sem(n) for n in ("h_ready", "gelu_done", "sq_done", "hi_done", "lo_done", "acc_done",
                             "acc_one", "proj_done"))
        stat_ready, post_step, post_pre, post_pow, p_sub, u_sub, x_sub = (
            sem(n) for n in ("stat_ready", "post_step", "post_pre", "post_pow", "p_sub", "u_sub", "x_sub"))
        gram_ready, gram_saved = sem("gram_ready"), sem("gram_saved")
        mu_saved = sem("mu_saved")
        qt_ready, qt_saved, q_ready, q_mul, q_add, q_saved = (
            sem(n) for n in ("qt_ready", "qt_saved", "q_ready", "q_mul", "q_add", "q_saved"))
        g_hi, g_lo, g_zero, gt_ready, gt_saved = (sem(n) for n in ("g_hi", "g_lo", "g_zero", "gt_ready", "gt_saved"))
        gu_ready, gu_saved, qd, red_ready, red_chain, s_pow, s_diag, s_row, s_saved = (
            sem(n) for n in ("gu_ready", "gu_saved", "quad_chain", "red_ready", "red_chain",
                             "s_pow", "s_diag", "s_row", "s_saved"))

        thr_p, sc_chain, sc_one = sem("thr_p"), sem("sc_chain"), sem("sc_one")

        POST = 8
        QD = 5 + 8 * (DC - 1)

        block = ctx.enter_context(nc.Block())

        @block.sync
        def _(sp):
            sp.dma_start(X[:, 0:SUB, :], x_v[:, 0:SUB, :]).then_inc(s_x[0], 16)
            for c in range(DC):
                sp.dma_start(wf_st[:, c, :], wf_v[:, c, :]).then_inc(s_wf[c], 16)
            for c in range(4):
                sp.dma_start(wp_st[c // 2][:, 4 * (c % 2):4 * (c % 2) + 4, :],
                             wp_v[:, 4 * c:4 * c + 4, :]).then_inc(s_wp[c], 16)
            with nc.allow_non_contiguous_dma(reason="the bias, one element per partition"):
                sp.dma_start(bcol[:], b_v).then_inc(s_b, 16)
            sp.dma_start(X[:, SUB:2 * SUB, :], x_v[:, SUB:2 * SUB, :]).then_inc(s_x[1], 16)
            sp.wait_ge(tern_f, 4)
            sp.dma_start(WT_st, WT_v[:, 0:8, :]).then_inc(s_WT, 16)
            sp.dma_start(W_st, W_v[:, :, 0:2 * D].rearrange("p c (j d) -> p c j d", j=2)).then_inc(s_W, 16)
            sp.wait_ge(tern_p, 4)
            for t in (2, 3):
                sp.dma_start(X[:, t * SUB:(t + 1) * SUB, :],
                             x_v[:, t * SUB:(t + 1) * SUB, :]).then_inc(s_x[t], 16)
            sp.wait_ge(ub_prod, 8)
            for t in range(4, NT):
                sp.dma_start(X[:, t * SUB:(t + 1) * SUB, :],
                             x_v[:, t * SUB:(t + 1) * SUB, :]).then_inc(s_x[t], 16)
            for o in range(NB):
                sp.wait_ge(gram_ready, DC * TPB * (o + 1))
                if o:
                    sp.wait_ge(qt_ready, SUB * 4)
                    sp.wait_ge(ln_lo["Q"], SUB * 4)
                for c in range(DC):
                    if c >= 2:
                        sp.wait_ge(qd, QD * o + 5 + 8 * (c - 2))
                    sp.dma_start(Wst[:, c % 2], W_v[:, c, :].rearrange("p (j d) -> p j d", j=3)
                                 ).then_inc(s_wst[c % 2], 16)
            with sp.Fori(0, NT - 1) as m:
                sp.wait_ge(x_sub, SUB * (m + NT + 1))
                sp.dma_start(out_v[:, bass.ts(m, SUB), :], X[:, bass.ts(m, SUB), :]).then_inc(out_stored, 16)
            for s in range(SUB):
                r = (NT - 1) * SUB + s
                sp.wait_ge(x_sub, SUB * (2 * NT - 1) + s + 1)
                sp.dma_start(out_v[:, r, :], X[:, r, :]).then_inc(out_stored, 16)
            sp.wait_ge(out_stored, 16 * (NT - 1 + SUB))

        @block.gpsimd
        def _(pool):
            nc.gpsimd.memset(half[:], -0.5).then_inc(const_ready, 1)
            nc.gpsimd.memset(ones32[:], 1.0).then_inc(const_ready, 1)
            nc.gpsimd.memset(ones16[:], 1.0).then_inc(const_ready, 1)
            nc.gpsimd.memset(id32[:], 0.0).then_inc(const_ready, 1)
            nc.gpsimd.memset(id16[:], 0.0).then_inc(const_ready, 1)
            pool.wait_ge(const_ready, 5)
            for m in (id32, id16):
                nc.gpsimd.affine_select(out=m[:], in_=m[:], compare_op=ALU.not_equal, fill=1.0, base=0,
                                        pattern=[[-1, P]], channel_multiplier=1).then_inc(const_ready, 1)

            def rsqrt(dst, src, pre, done, k, per=1):
                pool.wait_ge(pre, per * (k + 1))
                nc.gpsimd.tensor_tensor(dst[:], src[:], half[:], ALU.pow).then_inc(done, 1)

            def tile(n, gram, nxt):
                if gram:
                    rsqrt(pwA, veA, ln_pre["A"], ln_pow["A"], n - 1)
                if nxt:
                    rsqrt(pw, ve, ln_pre["F"], ln_pow["F"], n + 1)
                rsqrt(pwP, veP, post_pre, post_pow, n)

            rsqrt(pw, ve, ln_pre["F"], ln_pow["F"], 0)
            tile(0, False, True)
            with pool.Fori(1, TPB + 1) as n:
                tile(n, True, True)
            rsqrt(ip, prod, red_chain, s_pow, 0, 12)
            with pool.Fori(TPB + 1, NT - 1) as n:
                tile(n, True, True)
            with pool.Fori(NT - 1, NT + 1) as n:
                tile(n, True, True)
            with pool.Fori(NT + 1, NT + 3) as n:
                tile(n, False, True)
            rsqrt(ip, prod, red_chain, s_pow, 1, 12)
            with pool.Fori(NT + 3, 2 * NT - 1) as n:
                tile(n, False, True)
            tile(2 * NT - 1, False, False)

        @block.tensor
        def _(pe):
            def transposes(i, k, src, sm_lo, dst_bank, done, chunk=0):
                ps = dst_bank[:].bitcast(F16).rearrange("p (h c t) -> p h c t", h=2, c=DC)
                pe.wait_ge(sm_lo, SUB * k + i + 1)
                for h in range(2):
                    for c in range(DC):
                        last = nc.tensor.transpose(ps[:, h, c, :], src[:, h, i, c * P:(c + 1) * P], id16[:])
                last.then_inc(done, 1)

            def fc(n, b):
                B = FB * n + b
                wait(pe, gelu_done, B - 1)
                for c in range(DC):
                    for h in range(2):
                        last = nc.tensor.matmul(H[b % 2][:], wf[:, c, b * P:(b + 1) * P], xT[:, h, c, :],
                                                start=(c == 0 and h == 0), stop=(c == DC - 1 and h == 1))
                last.then_inc(h_ready, 1)

            def proj(n, b):
                pe.wait_ge(lo_done, FB * n + b + 1)
                if b == 0:
                    wait(pe, u_sub, SUB * n)
                for s in range(SUB):
                    for h in range(2):
                        last = nc.tensor.matmul(A[s][:], G2[:, b % LAG, h, s * P:(s + 1) * P], wp[:, b, :],
                                                start=(b == 0 and h == 0), stop=(b == FB - 1 and h == 1))
                    if b == FB - 1:
                        last.then_inc(p_sub, 1)
                if b < FB - 1:
                    last.then_inc(proj_done, 1)

            def gram(n, m):
                if m == 0:
                    pe.wait_ge(ln_lo["A"], SUB * n)
                    if n_has_q[0]:
                        pe.wait_ge(qt_saved, SUB * (n - (NT - 1)) + SUB)
                if m == 1 and n_has_q[0]:
                    pe.wait_ge(q_mul, SUB * (n - (NT - 1)) + SUB)
                if m >= 2:
                    pe.wait_ge(gram_saved, DC * (n - 1) + m - 1)
                w = D - m * P
                g = S[m % 2]
                for s in range(SUB):
                    for i, (l, r) in enumerate(((0, 0), (0, 1), (1, 0))):
                        last = nc.tensor.matmul(g[:, 0:w], hlA[:, l, s, m * P:(m + 1) * P],
                                                hlA[:, r, s, m * P:D],
                                                start=(s == 0 and i == 0), stop=(s == SUB - 1 and i == 2))
                if m == DC - 1:
                    for c in range(DC):
                        for s in range(SUB):
                            for h in range(2):
                                last = nc.tensor.matmul(g[:, 256 + c:257 + c], hlA[:, h, s, c * P:(c + 1) * P],
                                                        ones16[:, 0:1], start=(s == 0 and h == 0),
                                                        stop=(s == SUB - 1 and h == 1))
                last.then_inc(gram_ready, 1)

            def q_transpose(n, s):
                m = n - (NT - 1)
                if s:
                    pe.wait_ge(qt_saved, SUB * m + s)
                transposes(s, m, hlQ, ln_lo["Q"], S[0], qt_ready)

            def q_product(n, s):
                m = n - (NT - 1)
                pe.wait_ge(qt_saved, SUB * m + s + 1)
                if s:
                    pe.wait_ge(q_mul, SUB * m + s)
                for c in range(DC):
                    for i, (l, r) in enumerate(((0, 0), (0, 1), (1, 0))):
                        last = nc.tensor.matmul(S[1][:], qT[:, s % 2, l, c, :], U[:, 0, r, c, :],
                                                start=(c == 0 and i == 0), stop=(c == DC - 1 and i == 2))
                last.then_inc(q_ready, 1)

            n_has_q = [False]

            def tile(n, with_gram, with_q, nxt, hooks=None):
                n_has_q[0] = with_q
                for b in range(LAG):
                    if b == 0:
                        pe.wait_ge(t_saved, SUB * (n + 1))
                    if hooks:
                        hooks(b)
                    fc(n, b)
                for b in range(LAG, STEPS):
                    if hooks:
                        hooks(b)
                    fc(n, b)
                    if hooks and (b - LAG) % 4 == 0:
                        pe.wait_ge(tern_p, (b - LAG) // 4 + 1)
                    proj(n, b - LAG)
                    if with_q:
                        if 4 <= b < 8:
                            q_transpose(n, b - 4)
                        if 5 <= b < 9:
                            q_product(n, b - 5)
                    if with_gram and 9 <= b < 13:
                        gram(n, b - 9)
                for i in range(SUB):
                    if nxt:
                        if i < 2:
                            if with_gram:
                                pe.wait_ge(gram_saved, DC * (n - 1) + 3 + i)
                            elif with_q and i == 1:
                                pe.wait_ge(q_mul, SUB * (n - (NT - 1)) + SUB)
                            elif hooks:
                                pe.wait_ge(bn_saved, 2)
                        else:
                            pe.wait_ge(t_saved, SUB * (n + 1) + i - 1)
                        transposes(i, n + 1, hl, ln_lo["F"], S[i % 2], t_ready)
                    if i == SUB - 1:
                        stats(n, nxt)
                    if hooks and i == 0:
                        pe.wait_ge(tern_p, 4)
                    proj(n, FB - LAG + i)

            def stats(n, nxt):
                pe.wait_ge(acc_done, FB * (n + 1))
                if nxt:
                    pe.wait_ge(t_saved, SUB * (n + 1) + 3)
                for j, a in enumerate((acc1, acc2)):
                    for s in range(SUB):
                        last = nc.tensor.matmul(S[0][:, SUB * j + s:SUB * j + s + 1], a[:, s * P:(s + 1) * P],
                                                ones32[:, 0:1], start=True, stop=True)
                last.then_inc(stat_ready, 1)

            def quad(o, n):
                pe.wait_ge(g_lo, DC * (o + 1))
                pe.wait_ge(post_step, POST * (n + 1) - 4)
                pe.wait_ge(t_saved, SUB * (n + 2))
                for h in range(2):
                    ps = S[h][:].bitcast(F16)
                    k = 0
                    for i in range(DC - 1):
                        for j in range(i + 1, DC):
                            last = nc.tensor.transpose(ps[:, k * P:(k + 1) * P], GH[:, h, i, j * P:(j + 1) * P],
                                                       id16[:])
                            k += 1
                    last.then_inc(gt_ready, 1)
                pe.wait_ge(gt_saved, 2 * (o + 1))
                for m in range(DC):
                    for j, r in ((1, 0), (0, 1)):
                        if m:
                            pe.wait_ge(gu_saved, 2 * (DC * o + m - 1) + r + 1)
                        for c in range(DC):
                            for i, (l, h) in enumerate(((0, 0), (0, 1), (1, 0))):
                                last = nc.tensor.matmul(S[r][:], GH[:, l, c, m * P:(m + 1) * P], U[:, j, h, c, :],
                                                        start=(c == 0 and i == 0), stop=(c == DC - 1 and i == 2))
                        last.then_inc(gu_ready, 1)
                pe.wait_ge(qd, QD * (o + 1))
                for r in range(5):
                    a = sums[:, r, :] if r < 4 else sum_mq
                    for c in range(DC):
                        last = nc.tensor.matmul(S[0][:, DC * r + c:DC * r + c + 1], a[:, c * P:(c + 1) * P],
                                                ones32[:, 0:1], start=True, stop=True)
                last.then_inc(red_ready, 1)
                for j in range(2):
                    pe.wait_ge(s_diag, 2 * o + j + 1)
                    for c in range(DC):
                        last = nc.tensor.matmul(S[j][:, c * P:(c + 1) * P], ones32[:], diag[:, j, c, :],
                                                start=True, stop=True)
                    last.then_inc(s_row, 1)
                pe.wait_ge(s_saved, 2 * (o + 1))

            pe.wait_ge(const_ready, 7)
            for i in range(SUB):
                if i >= 2:
                    pe.wait_ge(t_saved, i - 1)
                transposes(i, 0, hl, ln_lo["F"], S[i % 2], t_ready)
            pe.wait_ge(abs_dve, 2)
            pe.wait_ge(abs_act, 2)
            nc.tensor.matmul(H[0][:, 0:4], ones32[:], absum[:, 0, :], start=True, stop=True
                             ).then_inc(total_ready, 1)

            def first(b):
                if b % 4 == 0:
                    pe.wait_ge(tern_f, b // 4 + 1)
                if b == 4:
                    pe.wait_ge(abs_dve, 4)
                    pe.wait_ge(abs_act, 4)
                    nc.tensor.matmul(A[0][:, 0:4], ones32[:], absum[:, 1, :], start=True, stop=True
                                     ).then_inc(total_ready, 1)
                    pe.wait_ge(scal, 8)
                if b in (8, 9):
                    j = b - 8
                    pe.wait_ge(ub_diag, j + 1)
                    for c in range(DC):
                        last = nc.tensor.matmul(S[j][:, c * P:(c + 1) * P], ones32[:], diag[:, j, c, :],
                                                start=True, stop=True)
                    last.then_inc(ub_row, 1)
                if b == 12:
                    pe.wait_ge(ub_prod, 8)
                    pe.wait_ge(tern_p, 4)
                    for c in range(FB):
                        last = nc.tensor.matmul(S[1][:], ones16[:], wp[:, c, :], start=(c == 0),
                                                stop=(c == FB - 1))
                    last.then_inc(tsum_ready, 1)
                if b == 14:
                    pe.wait_ge(tsum_saved, 1)
                    for j in range(2):
                        pe.wait_ge(ub_diag, 3 + j)
                        for c in range(DC):
                            last = nc.tensor.matmul(S[j][:, c * P:(c + 1) * P], ones32[:], diag[:, j, c, :],
                                                    start=True, stop=True)
                        last.then_inc(ub_row, 1)

            tile(0, False, False, True, first)
            with pe.Fori(1, TPB + 1) as n:
                tile(n, True, False, True)
            quad(0, TPB)
            with pe.Fori(TPB + 1, NT - 1) as n:
                tile(n, True, False, True)
            with pe.Fori(NT - 1, NT + 1) as n:
                tile(n, True, True, True)
            with pe.Fori(NT + 1, NT + 3) as n:
                tile(n, False, True, True)
            quad(1, NT + 2)
            with pe.Fori(NT + 3, 2 * NT - 1) as n:
                tile(n, False, True, True)
            tile(2 * NT - 1, False, False, False)

        @block.scalar
        def _(act):
            def ln_split(kind, k, s, dst):
                act.wait_ge(ln_v[kind], SUB * k + s + 1)
                nc.scalar.activation(dst[:, 0, s, :], vb[:, s % 2, :], ACT.Copy).then_inc(ln_hi[kind], 1)

            def save_transposed(i, k, dst, ready, done):
                act.wait_ge(ready, SUB * k + i + 1)
                nc.scalar.activation(dst, S[i % 2][:].bitcast(F16).rearrange("p (h c t) -> p h c t", h=2, c=DC),
                                     ACT.Copy).then_inc(done, 1)

            def gelu(n, b):
                B = FB * n + b
                act.wait_ge(h_ready, B + 1)
                wait(act, acc_done, B - 1)
                nc.scalar.activation(gf[:, b % 2, :], H[b % 2][:], ACT.Gelu, scale=hscale[:, 0:1]
                                     ).then_inc(gelu_done, 1)

            def split(n, b):
                B = FB * n + b
                act.wait_ge(gelu_done, B + 1)
                if b >= LAG:
                    act.wait_ge(proj_done, (FB - 1) * n + b - LAG + 1)
                else:
                    wait(act, p_sub, SUB * n)
                nc.scalar.activation(G2[:, b % LAG, 0, :], gf[:, b % 2, :], ACT.Copy, scale=kap[:, 0:1]
                                     ).then_inc(hi_done, 1)
                wait(act, acc_done, B - 1)
                nc.scalar.activation(sq[:, b % 2, :], gf[:, b % 2, :], ACT.Square).then_inc(sq_done, 1)

            def tile(n, with_gram, with_q, nxt, hooks=None):
                for b in range(STEPS + 1):
                    if b < STEPS:
                        gelu(n, b)
                    if b:
                        split(n, b - 1)
                    if hooks:
                        hooks(b)
                    if with_q:
                        if b in (0, 2):
                            for s in (b, b + 1):
                                ln_split("Q", n - (NT - 1), s, hlQ)
                        if 5 <= b < 9:
                            s = b - 5
                            m = n - (NT - 1)
                            act.wait_ge(qt_ready, SUB * m + s + 1)
                            if s >= 2:
                                act.wait_ge(q_ready, SUB * m + s - 1)
                            nc.scalar.activation(qT[:, s % 2], S[0][:].bitcast(F16).rearrange(
                                "p (h c t) -> p h c t", h=2, c=DC), ACT.Copy).then_inc(qt_saved, 1)
                    if with_gram and b in (6, 8):
                        for s in (b - 6, b - 5):
                            ln_split("A", n - 1, s, hlA)
                    if nxt and b in (13, 15):
                        for s in (b - 13, b - 12):
                            ln_split("F", n + 1, s, hl)
                if nxt:
                    for i in range(SUB):
                        if i == 0:
                            act.wait_ge(h_ready, FB * (n + 1))
                        save_transposed(i, n + 1, xT[:, :, :, i * P:(i + 1) * P], t_ready, t_saved)

            for s in range(SUB):
                ln_split("F", 0, s, hl)
            for i in range(SUB):
                save_transposed(i, 0, xT[:, :, :, i * P:(i + 1) * P], t_ready, t_saved)
            dump = G2[:].rearrange("p a h t -> p (a h t)")
            for c in (1, 3):
                act.wait_ge(s_wf[c], 16)
                nc.scalar.activation(dump[:, 1024 * (c - 1):1024 * (c + 1)], wf_st[:, c, :], ACT.Abs,
                                     accum_out=absum[:, 0, c:c + 1]).then_inc(abs_act, 1)
            act.wait_ge(abs_act, 2)
            for c in (1, 3):
                act.wait_ge(s_wp[c], 16)
                nc.scalar.activation(dump[:, 1024 * (c - 1):1024 * (c + 1)].rearrange("p (c d) -> p c d", d=D),
                                     wp_st[c // 2][:, 4 * (c % 2):4 * (c % 2) + 4, :], ACT.Abs,
                                     accum_out=absum[:, 1, c:c + 1]).then_inc(abs_act, 1)
            act.wait_ge(abs_act, 4)
            act.wait_ge(scal, 5)

            def first(b):
                if 9 <= b < 13:
                    for i in (2 * (b - 9), 2 * (b - 9) + 1):
                        act.wait_ge(ub_prod, i + 1)
                        nc.scalar.activation(U[:, i // 4, 0, i % 4, :], ub[:, i % 2, :], ACT.Copy
                                             ).then_inc(ub_hi, 1)

            tile(0, False, False, True, first)
            with act.Fori(1, TPB + 1) as n:
                tile(n, True, False, True)

            def quad(o):
                act.wait_ge(gt_ready, 2 * o + 1)
                k = 0
                for i in range(DC - 1):
                    w = DC - 1 - i
                    last = nc.scalar.activation(
                        GH[:, 0, i + 1:DC, i * P:(i + 1) * P],
                        S[0][:].bitcast(F16)[:, k * P:(k + w) * P].rearrange("p (c d) -> p c d", c=w), ACT.Copy)
                    k += w
                last.then_inc(gt_saved, 1)

            quad(0)
            with act.Fori(TPB + 1, NT - 1) as n:
                tile(n, True, False, True)
            with act.Fori(NT - 1, NT + 1) as n:
                tile(n, True, True, True)
            with act.Fori(NT + 1, NT + 3) as n:
                tile(n, False, True, True)
            quad(1)
            with act.Fori(NT + 3, 2 * NT - 1) as n:
                tile(n, False, True, True)
            tile(2 * NT - 1, False, False, False)

        @block.vector
        def _(dve):
            V = nc.vector

            def ln_stats(kind, k, s, row):
                V.bn_stats((st if kind == "F" else stA)[:, s, :], X[:, row, :]).then_inc(ln_stat[kind], 1)

            def ln_var(kind, k, t):
                stats = st if kind == "F" else stA
                A0 = 5 * k
                dve.wait_ge(ln_stat[kind], SUB * (k + 1))
                V.tensor_tensor(msum[:], stats[:, :, 1], stats[:, :, 4], ALU.add).then_inc(ln_aggr[kind], 1)
                V.tensor_tensor(mdif[:], stats[:, :, 1], stats[:, :, 4], ALU.subtract).then_inc(ln_aggr[kind], 1)
                V.tensor_tensor(vsum[:], stats[:, :, 2], stats[:, :, 5], ALU.add).then_inc(ln_aggr[kind], 1)
                dve.wait_ge(ln_aggr[kind], A0 + 2)
                V.scalar_tensor_tensor(vdif[:], mdif[:], D / 4.0, mdif[:], ALU.mult, ALU.mult
                                       ).then_inc(ln_aggr[kind], 1)
                mean = mF[:] if kind == "F" else mA[:, bass.ts(t, SUB)]
                V.tensor_scalar(mean, msum[:], 0.5, None, ALU.mult).then_inc(ln_mean[kind], 1)
                dve.wait_ge(ln_aggr[kind], A0 + 4)
                V.tensor_tensor(vtot[:], vsum[:], vdif[:], ALU.add).then_inc(ln_aggr[kind], 1)
                dve.wait_ge(ln_aggr[kind], A0 + 5)
                if kind == "A":
                    V.tensor_scalar(veA[:], vtot[:], 1.0 / D, EPS_LN, ALU.mult, ALU.add).then_inc(ln_pre["A"], 1)
                else:
                    V.tensor_scalar(ve[:], vtot[:], (1.0 + EPS_BIT) / D, EPS_LN * EPS_BIT, ALU.mult, ALU.add
                                    ).then_inc(ln_pre["F"], 1)
                    V.reciprocal(rz[:], vtot[:]).then_inc(ln_r["F"], 1)

            def ln_scale(kind, k, t):
                if kind == "A":
                    dve.wait_ge(ln_pow["A"], k + 1)
                    V.tensor_scalar(rA[:, bass.ts(t, SUB)], pwA[:], XS, None, ALU.mult).then_inc(ln_r["A"], 1)
                else:
                    dve.wait_ge(ln_r["F"], 3 * k + 1)
                    V.tensor_tensor(zz[:], rz[:], vtot[:], ALU.mult).then_inc(ln_r["F"], 1)
                    dve.wait_ge(ln_r["F"], 3 * k + 2)
                    dve.wait_ge(ln_pow["F"], k + 1)
                    V.scalar_tensor_tensor(rf[:], pw[:], XS, zz[:], ALU.mult, ALU.mult).then_inc(ln_r["F"], 1)

            def ln_rows(kind, k, s, t):
                if s >= 2:
                    dve.wait_ge(ln_hi[kind], SUB * k + s - 1)
                    dve.wait_ge(ln_lo[kind], SUB * k + s - 1)
                if kind == "F":
                    dve.wait_ge(ln_r["F"], 3 * (k + 1))
                    dve.wait_ge(ln_mean["F"], k + 1)
                    m, r = mF[:, s:s + 1], rf[:, s:s + 1]
                else:
                    if kind == "A":
                        dve.wait_ge(ln_r["A"], k + 1)
                        dve.wait_ge(ln_mean["A"], k + 1)
                    m, r = mA[:, bass.ds(SUB * t + s, 1)], rA[:, bass.ds(SUB * t + s, 1)]
                V.tensor_scalar(vb[:, s % 2, :], X[:, SUB * t + s, :], m, r, ALU.subtract, ALU.mult
                                ).then_inc(ln_v[kind], 1)

            def ln_low(kind, k, s, dst):
                dve.wait_ge(ln_hi[kind], SUB * k + s + 1)
                dve.wait_ge(ln_v[kind], SUB * k + s + 1)
                V.tensor_tensor(dst[:, 1, s, :], vb[:, s % 2, :], dst[:, 0, s, :], ALU.subtract
                                ).then_inc(ln_lo[kind], 1)

            def ln_step(kind, k, t, dst, j):
                if j == 1:
                    ln_low(kind, k, 0, dst)
                    ln_low(kind, k, 1, dst)
                if j == 2:
                    ln_low(kind, k, 2, dst)
                    ln_low(kind, k, 3, dst)
                if j < 2:
                    ln_rows(kind, k, 2 * j, t)
                    ln_rows(kind, k, 2 * j + 1, t)

            def hidden(n, b):
                B = FB * n + b
                dve.wait_ge(hi_done, B + 1)
                V.scalar_tensor_tensor(G2[:, b % LAG, 1, :], gf[:, b % 2, :], kap[:, 0:1], G2[:, b % LAG, 0, :],
                                       ALU.mult, ALU.subtract).then_inc(lo_done, 1)
                if b == 0:
                    V.tensor_copy(acc1[:], gf[:, 0, :]).then_inc(acc_one, 1)
                else:
                    dve.wait_ge(acc_one, B)
                    V.tensor_tensor(acc1[:], acc1[:], gf[:, b % 2, :], ALU.add).then_inc(acc_one, 1)
                dve.wait_ge(sq_done, B + 1)
                if b == 0:
                    V.tensor_copy(acc2[:], sq[:, 0, :]).then_inc(acc_done, 1)
                else:
                    dve.wait_ge(acc_done, B)
                    V.tensor_tensor(acc2[:], acc2[:], sq[:, b % 2, :], ALU.add).then_inc(acc_done, 1)

            def post_scalars(n):
                P0 = POST * n
                dve.wait_ge(stat_ready, n + 1)
                V.tensor_scalar(negm[:], S[0][:, 0:SUB], -1.0 / F, None, ALU.mult).then_inc(post_step, 1)
                V.tensor_scalar(negmk[:], S[0][:, 0:SUB], -1.0 / F, kap[:, 0:1], ALU.mult, ALU.mult
                                ).then_inc(post_step, 1)
                dve.wait_ge(post_step, P0 + 1)
                V.tensor_tensor(m2[:], negm[:], negm[:], ALU.mult).then_inc(post_step, 1)
                dve.wait_ge(post_step, P0 + 3)
                V.scalar_tensor_tensor(var[:], S[0][:, SUB:2 * SUB], 1.0 / F, m2[:], ALU.mult, ALU.subtract
                                       ).then_inc(post_step, 1)
                dve.wait_ge(post_step, P0 + 4)
                V.tensor_scalar(veP[:], var[:], 0.0, EPS_BIT, ALU.max, ALU.add).then_inc(post_pre, 1)
                V.tensor_scalar(varc[:], var[:], 0.0, None, ALU.max).then_inc(post_step, 1)
                dve.wait_ge(post_step, P0 + 5)
                V.reciprocal(rzP[:], varc[:]).then_inc(post_step, 1)
                dve.wait_ge(post_step, P0 + 6)
                V.tensor_tensor(zP[:], rzP[:], varc[:], ALU.mult).then_inc(post_step, 1)

            def post_rows(n, t):
                dve.wait_ge(post_step, POST * n + 7)
                dve.wait_ge(post_pow, n + 1)
                V.scalar_tensor_tensor(cP[:], pwP[:], cs[:, 0:1], zP[:], ALU.mult, ALU.mult
                                       ).then_inc(post_step, 1)
                for s in range(SUB + 1):
                    if s < SUB:
                        dve.wait_ge(p_sub, SUB * n + s + 1)
                        if s >= 2:
                            dve.wait_ge(x_sub, SUB * n + s - 1)
                        V.scalar_tensor_tensor(ub[:, s % 2, :], Tsum[:], negmk[:, s:s + 1], A[s][:],
                                               ALU.mult, ALU.add).then_inc(u_sub, 1)
                    if s:
                        dve.wait_ge(u_sub, SUB * n + s)
                        if s == 1:
                            dve.wait_ge(post_step, POST * (n + 1))
                        row = SUB * t + s - 1
                        V.scalar_tensor_tensor(X[:, row, :], ub[:, (s - 1) % 2, :], cP[:, s - 1:s], X[:, row, :],
                                               ALU.mult, ALU.add).then_inc(x_sub, 1)

            def gram_add(n, m):
                dve.wait_ge(gram_ready, DC * (n - 1) + m + 1)
                w = D - m * P
                if m == DC - 1:
                    V.scalar_tensor_tensor(mu[:], S[m % 2][:, 256:256 + DC], TS / XS, mu[:],
                                           ALU.mult, ALU.add).then_inc(mu_saved, 1)
                V.scalar_tensor_tensor(Gacc[:, m, m * P:D], S[m % 2][:, 0:w], GS / XS / XS, Gacc[:, m, m * P:D],
                                       ALU.mult, ALU.add).then_inc(gram_saved, 1)

            def q_add_rows(n, s):
                m = n - (NT - 1)
                row = SUB * m + s
                k = SUB * m + s
                dve.wait_ge(q_ready, k + 1)
                if s >= 2:
                    dve.wait_ge(q_saved, k - 1)
                V.tensor_tensor(ub[:, s % 2, :], S[1][:], Srow[:], ALU.mult).then_inc(q_mul, 1)
                V.tensor_tensor(X[:, row, :], X[:, row, :], Brow[:], ALU.add).then_inc(q_add, 1)
                dve.wait_ge(q_mul, k + 1)
                dve.wait_ge(q_add, k + 1)
                V.tensor_tensor(X[:, row, :], X[:, row, :], ub[:, s % 2, :], ALU.add).then_inc(q_saved, 1)

            def tile(n, with_gram, with_q, nxt, hooks=None):
                if with_q:
                    m = n - (NT - 1)
                    ln_step("Q", m, m, hlQ, 0)
                if hooks is None:
                    post_rows(n - 1, n - 1 if with_gram else n - 1 - NT)
                for b in range(STEPS):
                    if with_gram and b == 0:
                        dve.wait_ge(x_sub, SUB * n)
                    if with_q and 7 <= b < 11:
                        dve.wait_ge(q_saved, SUB * m + b - 6)
                    hidden(n, b)
                    if hooks:
                        hooks(b)
                    if with_q and b in (1, 3):
                        ln_step("Q", m, m, hlQ, (b + 1) // 2)
                    if with_gram:
                        if b == 0:
                            for s in range(SUB):
                                ln_stats("A", n - 1, s, SUB * (n - 1) + s)
                        if b == 1:
                            ln_var("A", n - 1, n - 1)
                        if b == 3:
                            ln_scale("A", n - 1, n - 1)
                        if b in (4, 6, 8):
                            ln_step("A", n - 1, n - 1, hlA, b // 2 - 2)
                        if 9 <= b < 13:
                            gram_add(n, b - 9)
                    if with_q and 4 <= b < 8:
                        q_add_rows(n, b - 4)
                    if nxt:
                        if 7 <= b < 11:
                            t = n + 1 - NT if with_q else n + 1
                            ln_stats("F", n + 1, b - 7, SUB * t + b - 7)
                        if b == 10:
                            ln_var("F", n + 1, t)
                        if b in (11, 13, 15):
                            if b == 11:
                                ln_scale("F", n + 1, t)
                            ln_step("F", n + 1, t, hl, (b - 11) // 2)
                post_scalars(n)

            V.memset(Gacc[:], 0.0).then_inc(g_zero, 1)
            V.memset(mu[:], 0.0).then_inc(g_zero, 1)
            dve.wait_ge(s_x[0], 16)
            for s in range(SUB):
                ln_stats("F", 0, s, s)
            ln_var("F", 0, 0)
            ln_scale("F", 0, 0)
            for j in range(3):
                ln_step("F", 0, 0, hl, j)
            for c in (0, 2):
                dve.wait_ge(s_wf[c], 16)
                V.tensor_reduce(absum[:, 0, c:c + 1], wf_st[:, c, :], AX.X, ALU.add, apply_absolute_value=True
                                ).then_inc(abs_dve, 1)

            def thresholds(j, total):
                dve.wait_ge(total_ready, j + 1)
                V.tensor_reduce(gam[:, j:j + 1], total, AX.X, ALU.add).then_inc(scal, 1)
                dve.wait_ge(scal, 1 if j == 0 else 7)
                V.tensor_scalar(gam[:, j:j + 1], gam[:, j:j + 1], 1.0 / (D * F), None, ALU.mult).then_inc(scal, 1)
                dve.wait_ge(scal, 2 if j == 0 else 8)
                V.tensor_scalar(theta[:, j, 0:1], gam[:, j:j + 1], EPS_BIT, 0.5, ALU.add, ALU.mult
                                ).then_inc(neg_ready, 1)
                V.tensor_scalar(theta[:, j, 1:2], gam[:, j:j + 1], EPS_BIT, -0.5, ALU.add, ALU.mult
                                ).then_inc(neg_ready, 1)
                dve.wait_ge(neg_ready, 2 * (j + 1))

            def ternary(j, i, src, dst, below, done):
                V.tensor_scalar(below, src, theta[:, j, 1:2], None, ALU.is_lt).then_inc(done[0], 1)
                dve.wait_ge(done[0], i + 1)
                V.scalar_tensor_tensor(dst, src, theta[:, j, 0:1], below, ALU.is_gt, ALU.subtract
                                       ).then_inc(done[1], 1)

            below_done = neg_ready

            thresholds(0, H[0][:, 0:4])
            dve.wait_ge(scal, 2)
            V.tensor_scalar(hscale[:], gam[:, 0:1], 1.0 / XS, None, ALU.mult).then_inc(scal, 1)
            V.tensor_scalar(kinv[:], gam[:, 0:1], 1.0 / 64, None, ALU.mult).then_inc(scal, 1)
            dve.wait_ge(scal, 4)
            V.reciprocal(kap[:], kinv[:]).then_inc(scal, 1)
            below = wp[:].rearrange("p c d -> p (c d)")[:, 0:2048].rearrange("p (c d) -> p c d", c=DC)
            for i in range(4):
                cols = slice(512 * i, 512 * (i + 1))
                wait(dve, tern_f, i)
                V.tensor_scalar(below, wf_st[:, :, cols], theta[:, 0, 1:2], None, ALU.is_lt
                                ).then_inc(below_done, 1)
                dve.wait_ge(below_done, 2 + i + 1)
                V.scalar_tensor_tensor(wf[:, :, cols], wf_st[:, :, cols], theta[:, 0, 0:1], below,
                                       ALU.is_gt, ALU.subtract).then_inc(tern_f, 1)
            for c in (0, 2):
                dve.wait_ge(s_wp[c], 16)
                V.tensor_reduce(absum[:, 1, c:c + 1], wp_st[c // 2][:, 4 * (c % 2):4 * (c % 2) + 4, :], AX.XY,
                                ALU.add, apply_absolute_value=True).then_inc(abs_dve, 1)
            dve.wait_ge(scal, 5)
            V.tensor_scalar(cs[:], gam[:, 0:1], 0.5 / 64, None, ALU.mult).then_inc(scal, 1)

            def first(b):
                if b == 0:
                    dve.wait_ge(total_ready, 2)
                    V.tensor_reduce(gam[:, 1:2], A[0][:, 0:4], AX.X, ALU.add).then_inc(scal, 1)
                    dve.wait_ge(scal, 7)
                    V.tensor_scalar(gam[:, 1:2], gam[:, 1:2], 1.0 / (D * F), None, ALU.mult).then_inc(scal, 1)
                    dve.wait_ge(scal, 8)
                    V.tensor_scalar(theta[:, 1, 0:1], gam[:, 1:2], EPS_BIT, 0.5, ALU.add, ALU.mult
                                    ).then_inc(thr_p, 1)
                    V.tensor_scalar(theta[:, 1, 1:2], gam[:, 1:2], EPS_BIT, -0.5, ALU.add, ALU.mult
                                    ).then_inc(thr_p, 1)
                    dve.wait_ge(scal, 6)
                    V.tensor_tensor(cs[:], cs[:], gam[:, 1:2], ALU.mult).then_inc(thr_p, 1)
                    dve.wait_ge(thr_p, 3)
                if b < 4:
                    i = b
                    src = wp_st[i // 2][:, 4 * (i % 2):4 * (i % 2) + 4, :]
                    lowv = bnrow[:].rearrange("p j d -> p (j d)").bitcast(F16).rearrange("p (c d) -> p c d", c=4)
                    wait(dve, tern_p, i)
                    V.tensor_scalar(lowv, src, theta[:, 1, 1:2], None, ALU.is_lt).then_inc(thr_p, 1)
                    dve.wait_ge(thr_p, 3 + i + 1)
                    V.scalar_tensor_tensor(wp[:, 4 * i:4 * i + 4, :], src, theta[:, 1, 0:1], lowv,
                                           ALU.is_gt, ALU.subtract).then_inc(tern_p, 1)
                if b == 4:
                    dve.wait_ge(s_WT, 16)
                    dve.wait_ge(s_b, 16)
                    V.tensor_reduce(acol[:], WT_st, AX.X, ALU.max, apply_absolute_value=True
                                    ).then_inc(ub_chain, 1)
                    V.tensor_reduce(babs[:], bcol[:, 0:8].rearrange("p (c a) -> p c a", a=1), AX.X, ALU.max,
                                    apply_absolute_value=True).then_inc(ub_chain, 1)
                    dve.wait_ge(ub_chain, 2)
                    V.tensor_tensor(acol[:], acol[:], babs[:], ALU.max).then_inc(ub_chain, 1)
                    dve.wait_ge(ub_chain, 3)
                    V.reciprocal(ra[:], acol[:]).then_inc(ub_chain, 1)
                    dve.wait_ge(ub_chain, 4)
                    V.tensor_scalar(raS[:], ra[:], US, None, ALU.mult).then_inc(ub_chain, 1)
                    V.tensor_tensor(bn[:], bcol[:, 0:8], ra[:], ALU.mult).then_inc(ub_chain, 1)
                    dve.wait_ge(ub_chain, 6)
                if b == 5:
                    for j in range(2):
                        for c in range(DC):
                            last = V.tensor_scalar(diag[:, j, c, :], id32[:], raS[:, 4 * j + c:4 * j + c + 1], None,
                                                   ALU.mult)
                        last.then_inc(ub_diag, 1)
                if 7 <= b < 11:
                    if b == 7:
                        dve.wait_ge(s_W, 16)
                    for i in (2 * (b - 7), 2 * (b - 7) + 1):
                        j, c = i // 4, i % 4
                        dve.wait_ge(ub_row, j + 1)
                        if i >= 2:
                            dve.wait_ge(ub_lo, i - 1)
                        V.tensor_tensor(ub[:, i % 2, :], S[j][:], W_st[:, c, j, :], ALU.mult
                                        ).then_inc(ub_prod, 1)
            def first_all(b):
                first_low(b)
                first(b)
                if b == 11:
                    for j in range(2):
                        dve.wait_ge(ub_row, j + 1)
                        for c in range(DC):
                            last = V.tensor_scalar(diag[:, j, c, :], id32[:], bn[:, 4 * j + c:4 * j + c + 1], None,
                                                   ALU.mult)
                        last.then_inc(ub_diag, 1)
                if b == 12:
                    dve.wait_ge(tsum_ready, 1)
                    V.tensor_copy(Tsum[:], S[1][:]).then_inc(tsum_saved, 1)
                if b == 15:
                    for j in range(2):
                        dve.wait_ge(ub_row, 3 + j)
                        V.tensor_copy(bnrow[:, j, :], S[j][:]).then_inc(bn_saved, 1)

            def first_low(b):
                if 8 <= b < 12:
                    for i in (2 * (b - 8), 2 * (b - 8) + 1):
                        dve.wait_ge(ub_hi, i + 1)
                        V.tensor_tensor(U[:, i // 4, 1, i % 4, :], ub[:, i % 2, :], U[:, i // 4, 0, i % 4, :],
                                        ALU.subtract).then_inc(ub_lo, 1)

            dve.wait_ge(s_x[1], 16)
            tile(0, False, False, True, first_all)
            for t in range(2, NT):
                dve.wait_ge(s_x[t], 16)
            dve.wait_ge(g_zero, 2)
            dve.wait_ge(tsum_saved, 1)
            with dve.Fori(1, TPB + 1) as n:
                tile(n, True, False, True)

            def quad(o):
                Q0 = QD * o
                dve.wait_ge(gram_saved, DC * TPB * (o + 1))
                for m in range(DC):
                    V.tensor_copy(GH[:, 0, m, m * P:D], Gacc[:, m, m * P:D]).then_inc(g_hi, 1)
                for m in range(DC):
                    dve.wait_ge(g_hi, DC * o + m + 1)
                    V.tensor_tensor(GH[:, 1, m, m * P:D], Gacc[:, m, m * P:D], GH[:, 0, m, m * P:D],
                                    ALU.subtract).then_inc(g_lo, 1)
                dve.wait_ge(gt_ready, 2 * (o + 1))
                k = 0
                for i in range(DC - 1):
                    w = DC - 1 - i
                    last = V.tensor_copy(GH[:, 1, i + 1:DC, i * P:(i + 1) * P],
                                         S[1][:].bitcast(F16)[:, k * P:(k + w) * P].rearrange("p (c d) -> p c d", c=w))
                    k += w
                last.then_inc(gt_saved, 1)
                step = [Q0]

                def did(ins):
                    step[0] += 1
                    ins.then_inc(qd, 1)
                    return step[0]

                made = {}
                for m in range(DC):
                    dve.wait_ge(s_wst[m % 2], 16 * (2 * o + m // 2 + 1))
                    wq_, wk_, wv_ = (Wst[:, m % 2, j, :] for j in range(3))
                    dve.wait_ge(gu_ready, 2 * (DC * o + m) + 1)
                    V.scalar_tensor_tensor(xk, bnrow[:, 1, :], mu[:, m:m + 1], S[0][:],
                                           ALU.mult, ALU.add).then_inc(gu_saved, 1)
                    dve.wait_ge(gu_saved, 2 * (DC * o + m) + 1)
                    for r, w in ((0, wk_), (1, wv_)):
                        if m == 0:
                            made[r] = did(V.tensor_tensor(sums[:, r, :], xk, w, ALU.mult))
                        else:
                            n1 = did(V.tensor_tensor(term[r], xk, w, ALU.mult))
                            dve.wait_ge(qd, n1)
                            made[r] = did(V.tensor_tensor(sums[:, r, :], sums[:, r, :], term[r], ALU.add))
                    if m == 0:
                        did(V.tensor_scalar(sums[:, 3, :], wk_, mu[:, 0:1], None, ALU.mult))
                    else:
                        did(V.scalar_tensor_tensor(sums[:, 3, :], wk_, mu[:, m:m + 1], sums[:, 3, :],
                                                   ALU.mult, ALU.add))
                    dve.wait_ge(gu_ready, 2 * (DC * o + m) + 2)
                    V.scalar_tensor_tensor(xq, bnrow[:, 0, :], mu[:, m:m + 1], S[1][:],
                                           ALU.mult, ALU.add).then_inc(gu_saved, 1)
                    dve.wait_ge(gu_saved, 2 * (DC * o + m) + 2)
                    if m == 0:
                        did(V.tensor_tensor(sums[:, 2, :], xq, wq_, ALU.mult))
                        did(V.tensor_scalar(sum_mq, wq_, mu[:, 0:1], None, ALU.mult))
                    else:
                        n1 = did(V.tensor_tensor(term[2], xq, wq_, ALU.mult))
                        dve.wait_ge(qd, n1)
                        did(V.tensor_tensor(sums[:, 2, :], sums[:, 2, :], term[2], ALU.add))
                        did(V.scalar_tensor_tensor(sum_mq, wq_, mu[:, m:m + 1], sum_mq, ALU.mult, ALU.add))
                assert step[0] - Q0 == QD, (step[0] - Q0, QD)
                dve.wait_ge(qd, Q0 + QD)
                V.memset(Gacc[:], 0.0).then_inc(g_zero, 1)
                V.memset(mu[:], 0.0).then_inc(g_zero, 1)
                dve.wait_ge(red_ready, o + 1)
                c0 = [12 * o]

                def chain(ins):
                    c0[0] += 1
                    ins.then_inc(red_chain, 1)
                    dve.wait_ge(red_chain, c0[0])

                r = lambda i: red[:, DC * i:DC * (i + 1)]
                chain(V.tensor_copy(red[:], S[0][:, 0:20]))
                chain(V.tensor_tensor(k1[:], r(3), ra[:, 4:8], ALU.mult))
                chain(V.scalar_tensor_tensor(k1[:], bn[:, 4:8], float(T * TS), k1[:], ALU.mult, ALU.add))
                chain(V.tensor_tensor(q1[:], r(4), ra[:, 0:4], ALU.mult))
                chain(V.scalar_tensor_tensor(q1[:], bn[:, 0:4], float(T * TS), q1[:], ALU.mult, ALU.add))
                chain(V.tensor_tensor(kk[:], bcol[:, 4:8], k1[:], ALU.mult))
                chain(V.tensor_tensor(kk[:], kk[:], r(0), ALU.add))
                chain(V.tensor_tensor(qq[:], bcol[:, 0:4], q1[:], ALU.mult))
                chain(V.tensor_tensor(qq[:], qq[:], r(2), ALU.add))
                chain(V.tensor_tensor(kk[:], kk[:], ra[:, 4:8], ALU.mult))
                chain(V.tensor_tensor(qq[:], qq[:], ra[:, 0:4], ALU.mult))
                chain(V.tensor_tensor(prod[:], kk[:], qq[:], ALU.mult))
                dve.wait_ge(s_pow, o + 1)
                return

            def quad_scale(o):
                r = lambda i: red[:, DC * i:DC * (i + 1)]
                c0 = [4 * o]

                def chain(ins):
                    c0[0] += 1
                    ins.then_inc(sc_chain, 1)
                    dve.wait_ge(sc_chain, c0[0])

                chain(V.tensor_tensor(kv[:], bcol[:, 8:12], k1[:], ALU.mult))
                chain(V.tensor_tensor(kv[:], kv[:], r(1), ALU.add))
                chain(V.tensor_tensor(sc2[:], kv[:], ip[:], ALU.mult))
                V.tensor_scalar(scol[:], sc2[:], 1.0 / (XS * US), None, ALU.mult).then_inc(sc_one, 1)
                chain(V.tensor_tensor(bsc[:], sc2[:], bn[:, 0:4], ALU.mult))
                dve.wait_ge(sc_one, o + 1)
                for j, col in ((0, scol), (1, bsc)):
                    for c in range(DC):
                        last = V.tensor_scalar(diag[:, j, c, :], id32[:], col[:, c:c + 1], None, ALU.mult)
                    last.then_inc(s_diag, 1)
                for j, row in ((0, Srow), (1, Brow)):
                    dve.wait_ge(s_row, 2 * o + j + 1)
                    V.tensor_copy(row[:], S[j][:]).then_inc(s_saved, 1)
                dve.wait_ge(s_saved, 2 * (o + 1))
                dve.wait_ge(g_zero, 2 * (o + 2))

            quad(0)
            quad_scale(0)
            with dve.Fori(TPB + 1, NT - 1) as n:
                tile(n, True, False, True)
            with dve.Fori(NT - 1, NT + 1) as n:
                tile(n, True, True, True)
            with dve.Fori(NT + 1, NT + 3) as n:
                tile(n, False, True, True)
            quad(1)
            quad_scale(1)
            with dve.Fori(NT + 3, 2 * NT - 1) as n:
                tile(n, False, True, True)
            tile(2 * NT - 1, False, False, False)
            post_rows(2 * NT - 1, NT - 1)


def kernel(L0_attn_x, L0_attn_W, L0_attn_b, L0_ffn_w_fc, L0_ffn_w_proj):
    import numpy as np
    import concourse.bacc as bacc
    from concourse.bass_utils import run_bass_kernel_spmd as run

    nc = bacc.Bacc("TRN2", target_bir_lowering=False, num_devices=1)
    arrays = {
        "x": np.ascontiguousarray(L0_attn_x),
        "WT": np.ascontiguousarray(np.transpose(L0_attn_W)),
        "W": np.ascontiguousarray(L0_attn_W),
        "b": np.ascontiguousarray(L0_attn_b),
        "wfT": np.ascontiguousarray(np.transpose(L0_ffn_w_fc)),
        "wpT": np.ascontiguousarray(np.transpose(L0_ffn_w_proj)),
    }
    args = [nc.dram_tensor(n, a.shape, F32, kind="ExternalInput").ap() for n, a in arrays.items()]
    out = nc.dram_tensor("out", arrays["x"].shape, F32, kind="ExternalOutput").ap()
    macaron_kernel(nc, *args, out)
    return run(nc, [arrays], core_ids=[0]).results[0]["out"]
```

```python
from contextlib import ExitStack

import concourse.bass as bass
from concourse import mybir

F32 = mybir.dt.float32
F16 = mybir.dt.float16
ALU = mybir.AluOpType
ACT = mybir.ActivationFunctionType
AX = mybir.AxisListType

P = 128
EPS_LN = 1e-5
EPS_BIT = 1e-6
XS = 2048.0
US = 1024.0
GS = 2.0 ** -5
TS = GS * US


def wait(eng, sem, value):
    if isinstance(value, int) and value <= 0:
        return
    eng.wait_ge(sem, value)


def macaron_kernel(nc, x, WT, W, b, wfT, wpT, out):
    NB, T, D = x.shape
    F = wfT.shape[1]
    DC = D // P
    FB = F // P
    SUB = 4
    TOK = SUB * P
    NT = NB * T // TOK
    TPB = T // TOK
    LAG = 4
    STEPS = FB
    NS = NT * SUB

    x_v = x.rearrange("b (s p) d -> p (b s) d", p=P)
    out_v = out.rearrange("b (s p) d -> p (b s) d", p=P)
    wf_v = wfT.rearrange("(c p) f -> p c f", p=P)
    wp_v = wpT.rearrange("(c p) o -> p c o", p=P)
    WT_v = WT.rearrange("(c p) d -> p c d", p=P)
    W_v = W.rearrange("(c p) n -> p c n", p=P)
    b_v = b.rearrange("(c p) -> p c", p=P)

    with ExitStack() as ctx:
        def sb(name, shape, dt=F32):
            return ctx.enter_context(nc.sbuf_tensor(name, shape, dt))

        def sem(name):
            return ctx.enter_context(nc.semaphore(name))

        X = sb("X", [P, NS, D])
        wf = sb("wf", [P, DC, F], F16)
        wp = sb("wp", [P, FB, D], F16)
        xT = sb("xT", [P, 2, DC, TOK], F16)
        qT = sb("qT", [P, 2, 2, DC, P], F16)
        G2 = sb("G2", [P, LAG, 2, TOK], F16)
        U = sb("U", [P, 2, 2, DC, D], F16)
        Gacc = sb("Gacc", [P, DC, D])
        acc1 = sb("acc1", [P, TOK])
        acc2 = sb("acc2", [P, TOK])
        Tsum = sb("Tsum", [P, D])
        Srow = sb("Srow", [P, D])
        Brow = sb("Brow", [P, D])
        low16 = sb("low16", [P, SUB, D], F16)
        ones32 = sb("ones32", [P, P])
        ones16 = sb("ones16", [P, P], F16)
        id32 = sb("id32", [P, P])
        id16 = sb("id16", [P, P], F16)
        scratch = sb("scratch", [P, 10240])

        def region(a, n, dt=F32):
            r = scratch[:, a:a + n]
            return r.bitcast(dt) if dt != F32 else r

        hl = region(0, 2048, F16).rearrange("p (h s d) -> p h s d", h=2, s=SUB)
        hlA = region(2048, 2048, F16).rearrange("p (h s d) -> p h s d", h=2, s=SUB)
        hlQ = region(4096, 2048, F16).rearrange("p (h s d) -> p h s d", h=2, s=SUB)
        gf = region(6144, 1024).rearrange("p (r t) -> p r t", r=2)
        sq = region(7168, 1024).rearrange("p (r t) -> p r t", r=2)
        vb = region(8192, 1024).rearrange("p (r t) -> p r t", r=2)
        ub = region(9216, 1024).rearrange("p (r t) -> p r t", r=2)
        sums = G2[:].rearrange("p a h t -> p (a h t)").bitcast(F32).rearrange("p (r t) -> p r t", r=4)
        more = region(8192, 1024).rearrange("p (r t) -> p r t", r=2)
        mu_sum = [sums[:, 3, :], more[:, 0, :], more[:, 1, :]]
        qT32 = qT[:].rearrange("p a h c t -> p (a h c t)").bitcast(F32)
        mu_term = [qT32[:, 0:512], qT32[:, 512:1024], region(9728, 512)]
        Wst = [region(a, 1536).rearrange("p (j d) -> p j d", j=3) for a in (2048, 0)]
        GH = region(6144, 2048, F16).rearrange("p (h c d) -> p h c d", h=2, c=DC)
        term = [region(a, 512) for a in (3584, 1536, 9216)]
        wf_st = X[:, 4 * SUB:8 * SUB, :].rearrange("p (c s) d -> p c (s d)", c=DC)
        wp_st = [X[:, 2 * SUB:4 * SUB, :], region(2048, 4096).rearrange("p (c d) -> p c d", d=D)]
        WT_st = X[:, 4 * SUB:6 * SUB, :]
        W_st = X[:, 6 * SUB:8 * SUB, :].rearrange("p (c j) d -> p c j d", c=DC)

        def small(name, *shape):
            return sb(name, [P, *shape])

        st = small("st", SUB, 6)
        stA = small("stA", SUB, 6)
        mF, msum, mdif, vsum, vdif, vtot = (small(n, SUB) for n in ("mF", "msum", "mdif", "vsum", "vdif", "vtot"))
        mA, nbF = small("mA", SUB), small("nbF", SUB)
        ve, pw, rz, zz, rf = (small(n, SUB) for n in ("ve", "pw", "rz", "zz", "rf"))
        veA, pwA = small("veA", SUB), small("pwA", SUB)
        rA, nbA = small("rA", NS), small("nbA", NS)
        negm, negmk, nmc, m2, var, varc, veP, pwP, rzP, zP, cP = (
            small(n, SUB) for n in ("negm", "negmk", "nmc", "m2", "var", "varc", "veP", "pwP", "rzP", "zP", "cP"))
        half = small("half", SUB)
        absum = small("absum", 2, 4)
        gam = small("gam", 2)
        theta = small("theta", 2, 2)
        hscale, kap, cs, kinv = (small(n, 1) for n in ("hscale", "kap", "cs", "kinv"))
        mu = small("mu", DC)
        bcol = small("bcol", 12)
        acol, babs, ra, bn, raS = (small(n, 8) for n in ("acol", "babs", "ra", "bn", "raS"))
        red = small("red", 24)
        k1, q1, k2, q2, kk, qq, kv, prod, ip, scol, bsc, sc2 = (
            small(n, DC) for n in ("k1", "q1", "k2", "q2", "kk", "qq", "kv", "prod", "ip", "scol", "bsc", "sc2"))
        diag = sb("diag", [P, 2, 4, P])

        def bank(name):
            return ctx.enter_context(nc.psum_tensor(name, [P, 512], F32))

        H = [bank("H0"), bank("H1")]
        A = [bank(f"A{s}") for s in range(SUB)]
        S = [bank("S0"), bank("S1")]

        QB = S + H

        s_x = [sem(f"x_loaded{t}") for t in range(NT)]
        s_wf = [sem(f"wf_loaded{c}") for c in range(DC)]
        s_wp = [sem(f"wp_loaded{c}") for c in range(4)]
        s_WT, s_W, s_b = sem("WT_loaded"), sem("W_loaded"), sem("b_loaded")
        s_wst = [sem("Wchunk_loaded0"), sem("Wchunk_loaded1")]
        out_stored = sem("out_stored")
        const_ready = sem("const_ready")
        abs_dve, abs_act = sem("abs_dve"), sem("abs_act")
        total_ready = sem("total_ready")
        scal = sem("scalars_chain")
        neg_ready = sem("neg_ready")
        tern_f, tern_p = sem("tern_f"), sem("tern_p")
        tsum_ready, tsum_saved = sem("tsum_ready"), sem("tsum_saved")
        ub_chain, ub_diag, ub_row, ub_prod, ub_hi, ub_lo = (
            sem(n) for n in ("u_chain", "u_diag", "u_row", "u_prod", "u_hi", "u_lo"))
        ln_stat, ln_aggr, ln_pre, ln_pow, ln_r, ln_v, ln_hi, ln_lo = (
            {k: sem(f"{n}{k}") for k in "FAQ"} for n in
            ("ln_stat", "ln_aggr", "ln_pre", "ln_pow", "ln_r", "ln_v", "ln_hi", "ln_lo"))
        ln_mean = {k: sem(f"ln_mean{k}") for k in "FA"}
        t_ready, t_saved = sem("t_ready"), sem("t_saved")
        h_ready, gelu_done, sq_done, hi_done, lo_done, acc_done, acc_one, proj_done = (
            sem(n) for n in ("h_ready", "gelu_done", "sq_done", "hi_done", "lo_done", "acc_done",
                             "acc_one", "proj_done"))
        stat_ready, post_step, post_pre, post_pow, p_sub, x_pre, x_sub = (
            sem(n) for n in ("stat_ready", "post_step", "post_pre", "post_pow", "p_sub", "x_pre", "x_sub"))
        gram_ready, gram_saved = sem("gram_ready"), sem("gram_saved")
        mu_saved = sem("mu_saved")
        qt_ready, qt_saved, q_ready, q_mul, q_add, q_saved = (
            sem(n) for n in ("qt_ready", "qt_saved", "q_ready", "q_mul", "q_add", "q_saved"))
        g_hi, g_lo, g_zero, gt_ready, gt_saved = (sem(n) for n in ("g_hi", "g_lo", "g_zero", "gt_ready", "gt_saved"))
        gu_ready, gu_saved, qd, red_ready, red_chain, s_pow, s_diag, s_row, s_saved = (
            sem(n) for n in ("gu_ready", "gu_saved", "quad_chain", "red_ready", "red_chain",
                             "s_pow", "s_diag", "s_row", "s_saved"))

        mw_prod, mw_ready = sem("mu_W_product"), sem("mu_W_sum")
        qt, red_saved = sem("quad_term"), sem("red_saved")
        thr_p, sc_chain, sc_one = sem("thr_p"), sem("sc_chain"), sem("sc_one")

        POST = 9
        QN = 1 + 3 * (DC - 1)
        RC = 15

        block = ctx.enter_context(nc.Block())

        @block.sync
        def _(sp):
            sp.dma_start(X[:, 0:SUB, :], x_v[:, 0:SUB, :]).then_inc(s_x[0], 16)
            for c in range(DC):
                sp.dma_start(wf_st[:, c, :], wf_v[:, c, :]).then_inc(s_wf[c], 16)
            for c in range(4):
                sp.dma_start(wp_st[c // 2][:, 4 * (c % 2):4 * (c % 2) + 4, :],
                             wp_v[:, 4 * c:4 * c + 4, :]).then_inc(s_wp[c], 16)
            with nc.allow_non_contiguous_dma(reason="the bias, one element per partition"):
                sp.dma_start(bcol[:], b_v).then_inc(s_b, 16)
            sp.dma_start(X[:, SUB:2 * SUB, :], x_v[:, SUB:2 * SUB, :]).then_inc(s_x[1], 16)
            sp.wait_ge(tern_f, 4)
            sp.dma_start(WT_st, WT_v[:, 0:8, :]).then_inc(s_WT, 16)
            sp.dma_start(W_st, W_v[:, :, 0:2 * D].rearrange("p c (j d) -> p c j d", j=2)).then_inc(s_W, 16)
            sp.wait_ge(tern_p, 4)
            for t in (2, 3):
                sp.dma_start(X[:, t * SUB:(t + 1) * SUB, :],
                             x_v[:, t * SUB:(t + 1) * SUB, :]).then_inc(s_x[t], 16)
            sp.wait_ge(ub_prod, 8)
            for t in range(4, NT):
                sp.dma_start(X[:, t * SUB:(t + 1) * SUB, :],
                             x_v[:, t * SUB:(t + 1) * SUB, :]).then_inc(s_x[t], 16)
            for o in range(NB):
                for c in range(DC):
                    if c == 0:
                        sp.wait_ge(gram_ready, DC * TPB * (o + 1))
                    if c == 1:
                        sp.wait_ge(t_ready, SUB * (TPB * (o + 1) + 2))
                    if c >= 2:
                        sp.wait_ge(gu_saved, 2 * (DC * o + c - 1))
                        sp.wait_ge(mw_prod, 3 * (DC * o + c - 1))
                    sp.dma_start(Wst[c % 2], W_v[:, DC - 1 - c, :].rearrange("p (j d) -> p j d", j=3)
                                 ).then_inc(s_wst[c % 2], 16)
            with sp.Fori(0, NT - 1) as m:
                sp.wait_ge(x_sub, SUB * (m + NT + 1))
                sp.dma_start(out_v[:, bass.ts(m, SUB), :], X[:, bass.ts(m, SUB), :]).then_inc(out_stored, 16)
            for s in range(SUB):
                r = (NT - 1) * SUB + s
                sp.wait_ge(x_sub, SUB * (2 * NT - 1) + s + 1)
                sp.dma_start(out_v[:, r, :], X[:, r, :]).then_inc(out_stored, 16)
            sp.wait_ge(out_stored, 16 * (NT - 1 + SUB))

        @block.gpsimd
        def _(pool):
            nc.gpsimd.memset(half[:], -0.5).then_inc(const_ready, 1)
            nc.gpsimd.memset(ones32[:], 1.0).then_inc(const_ready, 1)
            nc.gpsimd.memset(ones16[:], 1.0).then_inc(const_ready, 1)
            nc.gpsimd.memset(id32[:], 0.0).then_inc(const_ready, 1)
            nc.gpsimd.memset(id16[:], 0.0).then_inc(const_ready, 1)
            pool.wait_ge(const_ready, 5)
            for m in (id32, id16):
                nc.gpsimd.affine_select(out=m[:], in_=m[:], compare_op=ALU.not_equal, fill=1.0, base=0,
                                        pattern=[[-1, P]], channel_multiplier=1).then_inc(const_ready, 1)

            def rsqrt(dst, src, pre, done, k, per=1):
                pool.wait_ge(pre, per * (k + 1))
                nc.gpsimd.tensor_tensor(dst[:], src[:], half[:], ALU.pow).then_inc(done, 1)

            def tile(n, gram, nxt):
                if gram:
                    rsqrt(pwA, veA, ln_pre["A"], ln_pow["A"], n - 1)
                if nxt:
                    rsqrt(pw, ve, ln_pre["F"], ln_pow["F"], n + 1)
                rsqrt(pwP, veP, post_pre, post_pow, n)

            def quad(o):
                for g in range(1, DC):
                    for i in range(3):
                        pool.wait_ge(mw_prod, 3 * (DC * o + g) + i + 1)
                        if g > 1:
                            pool.wait_ge(mw_ready, 3 * ((DC - 1) * o + g - 2) + i + 1)
                        nc.gpsimd.tensor_tensor(mu_sum[i], mu_sum[i], mu_term[i], ALU.add).then_inc(mw_ready, 1)

            rsqrt(pw, ve, ln_pre["F"], ln_pow["F"], 0)
            tile(0, False, True)
            with pool.Fori(1, TPB + 1) as n:
                tile(n, True, True)
            quad(0)
            rsqrt(ip, prod, red_chain, s_pow, 0, RC)
            with pool.Fori(TPB + 1, NT - 1) as n:
                tile(n, True, True)
            with pool.Fori(NT - 1, NT + 1) as n:
                tile(n, True, True)
            quad(1)
            rsqrt(ip, prod, red_chain, s_pow, 1, RC)
            with pool.Fori(NT + 1, NT + 3) as n:
                tile(n, False, True)
            with pool.Fori(NT + 3, 2 * NT - 1) as n:
                tile(n, False, True)
            tile(2 * NT - 1, False, False)

        @block.tensor
        def _(pe):
            def transposes(i, k, src, sm_lo, dst_bank, done, chunk=0):
                ps = dst_bank[:].bitcast(F16).rearrange("p (h c t) -> p h c t", h=2, c=DC)
                pe.wait_ge(sm_lo, SUB * k + i + 1)
                for h in range(2):
                    for c in range(DC):
                        last = nc.tensor.transpose(ps[:, h, c, :], src[:, h, i, c * P:(c + 1) * P], id16[:])
                last.then_inc(done, 1)

            def fc(n, b):
                B = FB * n + b
                wait(pe, gelu_done, B - 1)
                for c in range(DC):
                    for h in range(2):
                        last = nc.tensor.matmul(H[b % 2][:], wf[:, c, b * P:(b + 1) * P], xT[:, h, c, :],
                                                start=(c == 0 and h == 0), stop=(c == DC - 1 and h == 1))
                last.then_inc(h_ready, 1)

            def proj(n, b):
                pe.wait_ge(lo_done, FB * n + b + 1)
                if b == 0:
                    wait(pe, x_sub, SUB * n)
                for s in range(SUB):
                    for h in range(2):
                        last = nc.tensor.matmul(A[s][:], G2[:, b % LAG, h, s * P:(s + 1) * P], wp[:, b, :],
                                                start=(b == 0 and h == 0), stop=(b == FB - 1 and h == 1))
                    if b == FB - 1:
                        last.then_inc(p_sub, 1)
                if b < FB - 1:
                    last.then_inc(proj_done, 1)

            def gram(n, m):
                if m == 0:
                    pe.wait_ge(ln_lo["A"], SUB * n)
                if m < 2 and n_has_q[0]:
                    pe.wait_ge(q_mul, SUB * (n - (NT - 1)) + 3 + m)
                if m >= 2:
                    pe.wait_ge(gram_saved, DC * (n - 1) + m - 1)
                w = D - m * P
                g = S[m % 2]
                for s in range(SUB):
                    for i, (l, r) in enumerate(((0, 0), (0, 1), (1, 0))):
                        last = nc.tensor.matmul(g[:, 0:w], hlA[:, l, s, m * P:(m + 1) * P],
                                                hlA[:, r, s, m * P:D],
                                                start=(s == 0 and i == 0), stop=(s == SUB - 1 and i == 2))
                if m == DC - 1:
                    for c in range(DC):
                        for s in range(SUB):
                            for h in range(2):
                                last = nc.tensor.matmul(g[:, 256 + c:257 + c], hlA[:, h, s, c * P:(c + 1) * P],
                                                        ones16[:, 0:1], start=(s == 0 and h == 0),
                                                        stop=(s == SUB - 1 and h == 1))
                last.then_inc(gram_ready, 1)

            def q_transpose(n, s):
                m = n - (NT - 1)
                if s >= 2:
                    pe.wait_ge(q_mul, SUB * m + s - 1)
                transposes(s, m, hlQ, ln_lo["Q"], S[s % 2], qt_ready)

            def q_product(n, s):
                m = n - (NT - 1)
                pe.wait_ge(qt_saved, SUB * m + s + 1)
                for c in range(DC):
                    for i, (l, r) in enumerate(((0, 0), (0, 1), (1, 0))):
                        last = nc.tensor.matmul(S[s % 2][:], qT[:, s % 2, l, c, :], U[:, 0, r, c, :],
                                                start=(c == 0 and i == 0), stop=(c == DC - 1 and i == 2))
                last.then_inc(q_ready, 1)

            n_has_q = [False]

            def tile(n, with_gram, with_q, nxt, hooks=None):
                n_has_q[0] = with_q
                if with_q:
                    pe.wait_ge(post_step, POST * (n - 1) + 4)
                    q_transpose(n, 0)
                    pe.wait_ge(t_saved, SUB * n + 2)
                    q_transpose(n, 1)
                for b in range(LAG):
                    if b == 0:
                        pe.wait_ge(t_saved, SUB * (n + 1))
                    if hooks:
                        hooks(b)
                    fc(n, b)
                    if with_q and b in (1, 2):
                        q_product(n, b - 1)
                for b in range(LAG, STEPS):
                    if hooks:
                        hooks(b)
                    fc(n, b)
                    if hooks and (b - LAG) % 4 == 0:
                        pe.wait_ge(tern_p, (b - LAG) // 4 + 1)
                    proj(n, b - LAG)
                    if with_q:
                        if b in (5, 6):
                            q_transpose(n, b - 3)
                        if b in (7, 8):
                            q_product(n, b - 5)
                    if with_gram and 10 <= b < 14:
                        gram(n, b - 10)
                for i in range(SUB):
                    if hooks and i == 0:
                        pe.wait_ge(tern_p, 4)
                    if i == 3:
                        stats(n, nxt)
                    proj(n, FB - LAG + i)
                    if nxt and i < 2:
                        if i == 0:
                            if with_gram:
                                pe.wait_ge(gram_saved, DC * n)
                            if with_q:
                                pe.wait_ge(q_mul, SUB * (n - (NT - 2)))
                            if hooks:
                                pe.wait_ge(tsum_saved, 1)
                        else:
                            pe.wait_ge(gelu_done, FB * (n + 1))
                        for j in (2 * i, 2 * i + 1):
                            transposes(j, n + 1, hl, ln_lo["F"], QB[j], t_ready)

            def stats(n, nxt):
                pe.wait_ge(acc_done, FB * (n + 1))
                if nxt:
                    pe.wait_ge(t_saved, SUB * (n + 1) + 1)
                for j, a in enumerate((acc1, acc2)):
                    for s in range(SUB):
                        last = nc.tensor.matmul(S[0][:, SUB * j + s:SUB * j + s + 1], a[:, s * P:(s + 1) * P],
                                                ones32[:, 0:1], start=True, stop=True)
                last.then_inc(stat_ready, 1)

            def quad(o, n):
                pe.wait_ge(g_lo, DC * (o + 1))
                pe.wait_ge(t_saved, SUB * (n + 2))
                pe.wait_ge(post_step, POST * n + 4)
                for h in range(2):
                    ps = S[h][:].bitcast(F16)
                    k = 0
                    for i in range(DC - 1):
                        for j in range(i + 1, DC):
                            last = nc.tensor.transpose(ps[:, k * P:(k + 1) * P], GH[:, h, i, j * P:(j + 1) * P],
                                                       id16[:])
                            k += 1
                    last.then_inc(gt_ready, 1)
                for g in range(DC):
                    m = DC - 1 - g
                    if g == 1:
                        pe.wait_ge(gt_saved, 2 * (o + 1))
                    for j, r in ((1, 0), (0, 1)):
                        r += 2 if g % 2 == 0 else 0
                        if g >= 2:
                            pe.wait_ge(gu_saved, 2 * (DC * o + g - 2) + r % 2 + 1)
                        for c in reversed(range(DC)) if g else range(DC):
                            first_c = DC - 1 if g else 0
                            last_c = DC - 1 - first_c
                            for i, (l, h) in enumerate(((0, 0), (0, 1), (1, 0))):
                                last = nc.tensor.matmul(QB[r][:], GH[:, l, c, m * P:(m + 1) * P], U[:, j, h, c, :],
                                                        start=(c == first_c and i == 0),
                                                        stop=(c == last_c and i == 2))
                        last.then_inc(gu_ready, 1)
                for r in (3, 4, 5, 0, 1, 2):
                    if r == 3:
                        pe.wait_ge(gu_saved, 2 * (DC * o + 2) + 2)
                        pe.wait_ge(mw_ready, 3 * (DC - 1) * (o + 1))
                    if r == 0:
                        pe.wait_ge(qd, QN * (o + 1))
                    a = sums[:, r, :] if r < 4 else more[:, r - 4, :]
                    for c in range(DC):
                        last = nc.tensor.matmul(H[0][:, DC * r + c:DC * r + c + 1], a[:, c * P:(c + 1) * P],
                                                ones32[:, 0:1], start=True, stop=True)
                last.then_inc(red_ready, 1)
                pe.wait_ge(red_saved, o + 1)

            def rows(o, n):
                pe.wait_ge(t_saved, SUB * (n + 2))
                pe.wait_ge(post_step, POST * n + 4)
                for j in range(2):
                    pe.wait_ge(s_diag, 2 * o + j + 1)
                    for c in range(DC):
                        last = nc.tensor.matmul(S[j][:, c * P:(c + 1) * P], ones32[:], diag[:, j, c, :],
                                                start=True, stop=True)
                    last.then_inc(s_row, 1)
                pe.wait_ge(s_saved, 2 * (o + 1))

            pe.wait_ge(const_ready, 7)
            for i in range(SUB):
                transposes(i, 0, hl, ln_lo["F"], QB[i], t_ready)
            pe.wait_ge(abs_dve, 2)
            pe.wait_ge(abs_act, 2)
            nc.tensor.matmul(A[1][:, 0:4], ones32[:], absum[:, 0, :], start=True, stop=True
                             ).then_inc(total_ready, 1)

            def first(b):
                if b % 4 == 0:
                    pe.wait_ge(tern_f, b // 4 + 1)
                if b == 4:
                    pe.wait_ge(abs_dve, 4)
                    pe.wait_ge(abs_act, 4)
                    nc.tensor.matmul(A[0][:, 0:4], ones32[:], absum[:, 1, :], start=True, stop=True
                                     ).then_inc(total_ready, 1)
                    pe.wait_ge(scal, 8)
                if b in (8, 9):
                    j = b - 8
                    pe.wait_ge(ub_diag, j + 1)
                    for c in range(DC):
                        last = nc.tensor.matmul(S[j][:, c * P:(c + 1) * P], ones32[:], diag[:, j, c, :],
                                                start=True, stop=True)
                    last.then_inc(ub_row, 1)
                if b == 12:
                    pe.wait_ge(ub_prod, 8)
                    pe.wait_ge(tern_p, 4)
                    for c in range(FB):
                        last = nc.tensor.matmul(S[1][:], ones16[:], wp[:, c, :], start=(c == 0),
                                                stop=(c == FB - 1))
                    last.then_inc(tsum_ready, 1)

            tile(0, False, False, True, first)
            with pe.Fori(1, TPB + 1) as n:
                tile(n, True, False, True)
            quad(0, TPB)
            with pe.Fori(TPB + 1, NT - 1) as n:
                tile(n, True, False, True)
            rows(0, NT - 2)
            with pe.Fori(NT - 1, NT + 1) as n:
                tile(n, True, True, True)
            quad(1, NT)
            with pe.Fori(NT + 1, NT + 3) as n:
                tile(n, False, True, True)
            rows(1, NT + 2)
            with pe.Fori(NT + 3, 2 * NT - 1) as n:
                tile(n, False, True, True)
            tile(2 * NT - 1, False, False, False)

        @block.scalar
        def _(act):
            def ln_wait(kind, k, half, before=None):
                if half:
                    act.wait_ge(ln_lo[kind], SUB * k + 2)
                else:
                    if kind == "F":
                        act.wait_ge(ln_r["F"], 4 * (k + 1))
                    elif kind == "A":
                        act.wait_ge(ln_r["A"], 2 * (k + 1))
                    if before:
                        act.wait_ge(*before)

            def ln_rows(kind, k, t, dst, half):
                buf = ub if kind == "Q" else vb
                for s in (2 * half, 2 * half + 1):
                    if kind == "F":
                        nb, r = nbF[:, s:s + 1], rf[:, s:s + 1]
                    else:
                        nb, r = nbA[:, bass.ds(SUB * t + s, 1)], rA[:, bass.ds(SUB * t + s, 1)]
                    nc.scalar.activation(buf[:, s % 2, :], X[:, SUB * t + s, :], ACT.Identity, bias=nb, scale=r
                                         ).then_inc(ln_v[kind], 1)
                for s in (2 * half, 2 * half + 1):
                    act.wait_ge(ln_v[kind], SUB * k + s + 1)
                    nc.scalar.activation(dst[:, 0, s, :], buf[:, s % 2, :], ACT.Copy).then_inc(ln_hi[kind], 1)

            def save_transposed(i, k, dst, ready, done):
                act.wait_ge(ready, SUB * k + i + 1)
                nc.scalar.activation(dst, QB[i][:].bitcast(F16).rearrange("p (h c t) -> p h c t", h=2, c=DC),
                                     ACT.Copy).then_inc(done, 1)

            def save_q(m, s):
                act.wait_ge(qt_ready, SUB * m + s + 1)
                if s >= 2:
                    act.wait_ge(q_ready, SUB * m + s - 1)
                nc.scalar.activation(qT[:, s % 2], S[s % 2][:].bitcast(F16).rearrange(
                    "p (h c t) -> p h c t", h=2, c=DC), ACT.Copy).then_inc(qt_saved, 1)

            def gelu(n, b):
                B = FB * n + b
                act.wait_ge(h_ready, B + 1)
                wait(act, acc_done, B - 1)
                nc.scalar.activation(gf[:, b % 2, :], H[b % 2][:], ACT.Gelu, scale=hscale[:, 0:1]
                                     ).then_inc(gelu_done, 1)

            def split(n, b, rows):
                B = FB * n + b
                act.wait_ge(gelu_done, B + 1)
                if b >= LAG:
                    act.wait_ge(proj_done, (FB - 1) * n + b - LAG + 1)
                else:
                    wait(act, p_sub, SUB * n)
                nc.scalar.activation(G2[:, b % LAG, 0, :], gf[:, b % 2, :], ACT.Copy, scale=kap[:, 0:1]
                                     ).then_inc(hi_done, 1)
                wait(act, acc_done, B - 1)
                if rows:
                    kind, k, t, dst, half, before = rows
                    ln_wait(kind, k, half, before)
                nc.scalar.activation(sq[:, b % 2, :], gf[:, b % 2, :], ACT.Square).then_inc(sq_done, 1)

            def tile(n, with_gram, with_q, nxt, hooks=None, next_q=True):
                m = n - (NT - 1)
                t = n + 1 - NT if with_q else n + 1
                for b in range(STEPS + 1):
                    if with_q and b == 0:
                        save_q(m, 0)
                        save_q(m, 1)
                    if b < STEPS:
                        gelu(n, b)
                    rows = []
                    if with_q and next_q and b in (10, 12):
                        rows = ["Q", m + 1, m + 1, hlQ, (b - 10) // 2, (q_saved, SUB * (m + 1))]
                    if with_gram and b in (4, 6):
                        rows = ["A", n - 1, n - 1, hlA, (b - 4) // 2, (ln_lo["F"], SUB * (n + 1))]
                    if nxt and b in (11, 13):
                        rows = ["F", n + 1, t, hl, (b - 11) // 2,
                                (ln_lo["A"], SUB * n) if with_gram else (ln_lo["F"], SUB * (n + 1))]
                    if b:
                        split(n, b - 1, rows)
                    if rows:
                        ln_rows(*rows[:-1])
                    if hooks:
                        hooks(b)
                    if with_q:
                        if b in (6, 7):
                            save_q(m, b - 4)
                if nxt:
                    for i in range(SUB):
                        if i == 0:
                            act.wait_ge(h_ready, FB * (n + 1))
                        save_transposed(i, n + 1, xT[:, :, :, i * P:(i + 1) * P], t_ready, t_saved)

            act.wait_ge(s_x[0], 16)
            for j in range(2):
                ln_wait("F", 0, j)
                ln_rows("F", 0, 0, hl, j)
            for i in range(SUB):
                save_transposed(i, 0, xT[:, :, :, i * P:(i + 1) * P], t_ready, t_saved)
            dump = G2[:].rearrange("p a h t -> p (a h t)")
            for c in (1, 3):
                act.wait_ge(s_wf[c], 16)
                nc.scalar.activation(dump[:, 1024 * (c - 1):1024 * (c + 1)], wf_st[:, c, :], ACT.Abs,
                                     accum_out=absum[:, 0, c:c + 1]).then_inc(abs_act, 1)
            act.wait_ge(abs_act, 2)
            for c in (1, 3):
                act.wait_ge(s_wp[c], 16)
                nc.scalar.activation(dump[:, 1024 * (c - 1):1024 * (c + 1)].rearrange("p (c d) -> p c d", d=D),
                                     wp_st[c // 2][:, 4 * (c % 2):4 * (c % 2) + 4, :], ACT.Abs,
                                     accum_out=absum[:, 1, c:c + 1]).then_inc(abs_act, 1)
            act.wait_ge(abs_act, 4)
            act.wait_ge(scal, 5)

            def first(b):
                if 9 <= b < 13:
                    for i in (2 * (b - 9), 2 * (b - 9) + 1):
                        act.wait_ge(ub_prod, i + 1)
                        nc.scalar.activation(U[:, i // 4, 0, i % 4, :], ub[:, i % 2, :], ACT.Copy
                                             ).then_inc(ub_hi, 1)

            act.wait_ge(s_x[1], 16)
            tile(0, False, False, True, first)
            for t in range(2, NT):
                act.wait_ge(s_x[t], 16)
            with act.Fori(1, TPB + 1) as n:
                tile(n, True, False, True)

            def quad(o):
                act.wait_ge(gt_ready, 2 * o + 1)
                k = 0
                for i in range(DC - 1):
                    w = DC - 1 - i
                    last = nc.scalar.activation(
                        GH[:, 0, i + 1:DC, i * P:(i + 1) * P],
                        S[0][:].bitcast(F16)[:, k * P:(k + w) * P].rearrange("p (c d) -> p c d", c=w), ACT.Copy)
                    k += w
                last.then_inc(gt_saved, 1)
                for g in range(DC):
                    m = DC - 1 - g
                    if g == 0:
                        act.wait_ge(mu_saved, TPB * (o + 1))
                        act.wait_ge(ln_lo["F"], SUB * (TPB * (o + 1) + 2))
                    act.wait_ge(s_wst[g % 2], 16 * (2 * o + g // 2 + 1))
                    for i, j in enumerate((1, 2, 0)):
                        if g > 1:
                            act.wait_ge(mw_ready, 3 * ((DC - 1) * o + g - 2) + i + 1)
                        nc.scalar.activation((mu_sum if g == 0 else mu_term)[i], Wst[g % 2][:, j, :], ACT.Copy,
                                             scale=mu[:, m:m + 1]).then_inc(mw_prod, 1)

            quad(0)
            with act.Fori(TPB + 1, NT - 1) as n:
                tile(n, True, False, True)
            for j in range(2):
                ln_wait("Q", 0, j)
                ln_rows("Q", 0, 0, hlQ, j)
            with act.Fori(NT - 1, NT + 1) as n:
                tile(n, True, True, True)
            quad(1)
            with act.Fori(NT + 1, NT + 3) as n:
                tile(n, False, True, True)
            with act.Fori(NT + 3, 2 * NT - 2) as n:
                tile(n, False, True, True)
            tile(2 * NT - 2, False, True, True, next_q=False)
            tile(2 * NT - 1, False, False, False)

        @block.vector
        def _(dve):
            V = nc.vector

            def ln_stats(kind, k, s, row):
                V.bn_stats((st if kind == "F" else stA)[:, s, :], X[:, row, :]).then_inc(ln_stat[kind], 1)

            def ln_var(kind, k, t):
                stats = st if kind == "F" else stA
                A0 = 5 * k
                dve.wait_ge(ln_stat[kind], SUB * (k + 1))
                V.tensor_tensor(msum[:], stats[:, :, 1], stats[:, :, 4], ALU.add).then_inc(ln_aggr[kind], 1)
                V.tensor_tensor(mdif[:], stats[:, :, 1], stats[:, :, 4], ALU.subtract).then_inc(ln_aggr[kind], 1)
                V.tensor_tensor(vsum[:], stats[:, :, 2], stats[:, :, 5], ALU.add).then_inc(ln_aggr[kind], 1)
                dve.wait_ge(ln_aggr[kind], A0 + 2)
                V.scalar_tensor_tensor(vdif[:], mdif[:], D / 4.0, mdif[:], ALU.mult, ALU.mult
                                       ).then_inc(ln_aggr[kind], 1)
                mean = mF[:] if kind == "F" else mA[:]
                V.tensor_scalar(mean, msum[:], 0.5, None, ALU.mult).then_inc(ln_mean[kind], 1)
                dve.wait_ge(ln_aggr[kind], A0 + 4)
                V.tensor_tensor(vtot[:], vsum[:], vdif[:], ALU.add).then_inc(ln_aggr[kind], 1)
                dve.wait_ge(ln_aggr[kind], A0 + 5)
                if kind == "A":
                    V.tensor_scalar(veA[:], vtot[:], 1.0 / D, EPS_LN, ALU.mult, ALU.add).then_inc(ln_pre["A"], 1)
                else:
                    V.tensor_scalar(ve[:], vtot[:], (1.0 + EPS_BIT) / D, EPS_LN * EPS_BIT, ALU.mult, ALU.add
                                    ).then_inc(ln_pre["F"], 1)
                    V.reciprocal(rz[:], vtot[:]).then_inc(ln_r["F"], 1)

            def ln_scale(kind, k, t):
                if kind == "A":
                    dve.wait_ge(ln_pow["A"], k + 1)
                    V.tensor_scalar(rA[:, bass.ts(t, SUB)], pwA[:], XS, None, ALU.mult).then_inc(ln_r["A"], 1)
                    dve.wait_ge(ln_r["A"], 2 * k + 1)
                    dve.wait_ge(ln_mean["A"], k + 1)
                    V.scalar_tensor_tensor(nbA[:, bass.ts(t, SUB)], mA[:], -1.0, rA[:, bass.ts(t, SUB)],
                                           ALU.mult, ALU.mult).then_inc(ln_r["A"], 1)
                else:
                    dve.wait_ge(ln_r["F"], 4 * k + 1)
                    V.tensor_tensor(zz[:], rz[:], vtot[:], ALU.mult).then_inc(ln_r["F"], 1)
                    dve.wait_ge(ln_r["F"], 4 * k + 2)
                    dve.wait_ge(ln_pow["F"], k + 1)
                    V.scalar_tensor_tensor(rf[:], pw[:], XS, zz[:], ALU.mult, ALU.mult).then_inc(ln_r["F"], 1)
                    dve.wait_ge(ln_r["F"], 4 * k + 3)
                    dve.wait_ge(ln_mean["F"], k + 1)
                    V.scalar_tensor_tensor(nbF[:], mF[:], -1.0, rf[:], ALU.mult, ALU.mult).then_inc(ln_r["F"], 1)

            def ln_low(kind, k, s, dst):
                buf = ub if kind == "Q" else vb
                dve.wait_ge(ln_hi[kind], SUB * k + s + 1)
                dve.wait_ge(ln_v[kind], SUB * k + s + 1)
                V.tensor_tensor(dst[:, 1, s, :], buf[:, s % 2, :], dst[:, 0, s, :], ALU.subtract
                                ).then_inc(ln_lo[kind], 1)

            def ln_lows(kind, k, half, dst):
                ln_low(kind, k, 2 * half, dst)
                ln_low(kind, k, 2 * half + 1, dst)

            def hidden(n, b):
                B = FB * n + b
                dve.wait_ge(hi_done, B + 1)
                V.scalar_tensor_tensor(G2[:, b % LAG, 1, :], gf[:, b % 2, :], kap[:, 0:1], G2[:, b % LAG, 0, :],
                                       ALU.mult, ALU.subtract).then_inc(lo_done, 1)
                if b == 0:
                    V.tensor_copy(acc1[:], gf[:, 0, :]).then_inc(acc_one, 1)
                else:
                    dve.wait_ge(acc_one, B)
                    V.tensor_tensor(acc1[:], acc1[:], gf[:, b % 2, :], ALU.add).then_inc(acc_one, 1)
                dve.wait_ge(sq_done, B + 1)
                if b == 0:
                    V.tensor_copy(acc2[:], sq[:, 0, :]).then_inc(acc_done, 1)
                else:
                    dve.wait_ge(acc_done, B)
                    V.tensor_tensor(acc2[:], acc2[:], sq[:, b % 2, :], ALU.add).then_inc(acc_done, 1)

            def post_scalars(n):
                P0 = POST * n
                dve.wait_ge(stat_ready, n + 1)
                V.tensor_scalar(negm[:], S[0][:, 0:SUB], -1.0 / F, None, ALU.mult).then_inc(post_step, 1)
                V.tensor_scalar(negmk[:], S[0][:, 0:SUB], -1.0 / F, kap[:, 0:1], ALU.mult, ALU.mult
                                ).then_inc(post_step, 1)
                dve.wait_ge(post_step, P0 + 1)
                V.tensor_tensor(m2[:], negm[:], negm[:], ALU.mult).then_inc(post_step, 1)
                dve.wait_ge(post_step, P0 + 3)
                V.scalar_tensor_tensor(var[:], S[0][:, SUB:2 * SUB], 1.0 / F, m2[:], ALU.mult, ALU.subtract
                                       ).then_inc(post_step, 1)
                dve.wait_ge(post_step, P0 + 4)
                V.tensor_scalar(veP[:], var[:], 0.0, EPS_BIT, ALU.max, ALU.add).then_inc(post_pre, 1)
                V.tensor_scalar(varc[:], var[:], 0.0, None, ALU.max).then_inc(post_step, 1)
                dve.wait_ge(post_step, P0 + 5)
                V.reciprocal(rzP[:], varc[:]).then_inc(post_step, 1)
                dve.wait_ge(post_step, P0 + 6)
                V.tensor_tensor(zP[:], rzP[:], varc[:], ALU.mult).then_inc(post_step, 1)

            def post_rows(n, t):
                dve.wait_ge(post_step, POST * n + 7)
                dve.wait_ge(post_pow, n + 1)
                V.scalar_tensor_tensor(cP[:], pwP[:], cs[:, 0:1], zP[:], ALU.mult, ALU.mult
                                       ).then_inc(post_step, 1)
                dve.wait_ge(post_step, POST * n + 8)
                V.tensor_tensor(nmc[:], negmk[:], cP[:], ALU.mult).then_inc(post_step, 1)
                dve.wait_ge(post_step, POST * (n + 1))
                for s in range(SUB):
                    row = SUB * t + s
                    V.scalar_tensor_tensor(X[:, row, :], Tsum[:], nmc[:, s:s + 1], X[:, row, :],
                                           ALU.mult, ALU.add).then_inc(x_pre, 1)
                post_product(n, t, 0)

            def post_product(n, t, pair):
                for s in (2 * pair, 2 * pair + 1):
                    row = SUB * t + s
                    dve.wait_ge(x_pre, SUB * n + s + 1)
                    dve.wait_ge(p_sub, SUB * n + s + 1)
                    V.scalar_tensor_tensor(X[:, row, :], A[s][:], cP[:, s:s + 1], X[:, row, :],
                                           ALU.mult, ALU.add).then_inc(x_sub, 1)

            def gram_add(n, m):
                dve.wait_ge(gram_ready, DC * (n - 1) + m + 1)
                w = D - m * P
                if m == DC - 1:
                    V.scalar_tensor_tensor(mu[:], S[m % 2][:, 256:256 + DC], TS / XS, mu[:],
                                           ALU.mult, ALU.add).then_inc(mu_saved, 1)
                V.scalar_tensor_tensor(Gacc[:, m, m * P:D], S[m % 2][:, 0:w], GS / XS / XS, Gacc[:, m, m * P:D],
                                       ALU.mult, ALU.add).then_inc(gram_saved, 1)

            def q_add_rows(n, s):
                m = n - (NT - 1)
                row = SUB * m + s
                k = SUB * m + s
                dve.wait_ge(q_ready, k + 1)
                if s >= 2:
                    dve.wait_ge(q_saved, k - 1)
                V.tensor_tensor(ub[:, s % 2, :], S[s % 2][:], Srow[:], ALU.mult).then_inc(q_mul, 1)
                V.tensor_tensor(X[:, row, :], X[:, row, :], Brow[:], ALU.add).then_inc(q_add, 1)
                dve.wait_ge(q_mul, k + 1)
                dve.wait_ge(q_add, k + 1)
                V.tensor_tensor(X[:, row, :], X[:, row, :], ub[:, s % 2, :], ALU.add).then_inc(q_saved, 1)

            def tile(n, with_gram, with_q, nxt, hooks=None, next_q=True, post=True):
                m = n - (NT - 1)
                t = n + 1 - NT if with_q else n + 1
                t_last = n - 1 if with_gram else n - 1 - NT
                if post:
                    post_rows(n - 1, t_last)
                for b in range(STEPS):
                    if with_gram and b < 2:
                        dve.wait_ge(x_sub, SUB * (n - 1) + 2 * (b + 1))
                    if with_q and b in (5, 9):
                        dve.wait_ge(q_saved, SUB * m + (2 if b == 5 else 4))
                    if nxt and b == 10:
                        ln_scale("F", n + 1, t)
                    hidden(n, b)
                    if post and b == 0:
                        post_product(n - 1, t_last, 1)
                    if hooks:
                        hooks(b)
                    if with_q:
                        if next_q and b in (10, 12):
                            ln_lows("Q", m + 1, (b - 10) // 2, hlQ)
                        if b in (2, 3, 7, 8):
                            q_add_rows(n, (2, 3, 7, 8).index(b))
                    if with_gram:
                        if b < 2:
                            for s in (2 * b, 2 * b + 1):
                                ln_stats("A", n - 1, s, SUB * (n - 1) + s)
                        if b == 1:
                            ln_var("A", n - 1, n - 1)
                        if b == 2:
                            ln_scale("A", n - 1, n - 1)
                        if b in (4, 6):
                            ln_lows("A", n - 1, (b - 4) // 2, hlA)
                        if 10 <= b < 14:
                            gram_add(n, b - 10)
                    if nxt:
                        s01, s23 = (5, 9) if with_q else (7, 8)
                        if b in (s01, s23):
                            for s in ((0, 1) if b == s01 else (2, 3)):
                                ln_stats("F", n + 1, s, SUB * t + s)
                        if b == s23:
                            ln_var("F", n + 1, t)
                        if b in (11, 13):
                            ln_lows("F", n + 1, (b - 11) // 2, hl)
                post_scalars(n)

            V.memset(Gacc[:], 0.0).then_inc(g_zero, 1)
            V.memset(mu[:], 0.0).then_inc(g_zero, 1)
            dve.wait_ge(s_x[0], 16)
            for s in range(SUB):
                ln_stats("F", 0, s, s)
            ln_var("F", 0, 0)
            ln_scale("F", 0, 0)
            for j in range(2):
                ln_lows("F", 0, j, hl)
            for c in (0, 2):
                dve.wait_ge(s_wf[c], 16)
                V.tensor_reduce(absum[:, 0, c:c + 1], wf_st[:, c, :], AX.X, ALU.add, apply_absolute_value=True
                                ).then_inc(abs_dve, 1)

            def thresholds(j, total):
                dve.wait_ge(total_ready, j + 1)
                V.tensor_reduce(gam[:, j:j + 1], total, AX.X, ALU.add).then_inc(scal, 1)
                dve.wait_ge(scal, 1 if j == 0 else 7)
                V.tensor_scalar(gam[:, j:j + 1], gam[:, j:j + 1], 1.0 / (D * F), None, ALU.mult).then_inc(scal, 1)
                dve.wait_ge(scal, 2 if j == 0 else 8)
                V.tensor_scalar(theta[:, j, 0:1], gam[:, j:j + 1], EPS_BIT, 0.5, ALU.add, ALU.mult
                                ).then_inc(neg_ready, 1)
                V.tensor_scalar(theta[:, j, 1:2], gam[:, j:j + 1], EPS_BIT, -0.5, ALU.add, ALU.mult
                                ).then_inc(neg_ready, 1)
                dve.wait_ge(neg_ready, 2 * (j + 1))

            def ternary(j, i, src, dst, below, done):
                V.tensor_scalar(below, src, theta[:, j, 1:2], None, ALU.is_lt).then_inc(done[0], 1)
                dve.wait_ge(done[0], i + 1)
                V.scalar_tensor_tensor(dst, src, theta[:, j, 0:1], below, ALU.is_gt, ALU.subtract
                                       ).then_inc(done[1], 1)

            below_done = neg_ready

            thresholds(0, A[1][:, 0:4])
            dve.wait_ge(scal, 2)
            V.tensor_scalar(hscale[:], gam[:, 0:1], 1.0 / XS, None, ALU.mult).then_inc(scal, 1)
            V.tensor_scalar(kinv[:], gam[:, 0:1], 1.0 / 64, None, ALU.mult).then_inc(scal, 1)
            dve.wait_ge(scal, 4)
            V.reciprocal(kap[:], kinv[:]).then_inc(scal, 1)
            below = wp[:].rearrange("p c d -> p (c d)")[:, 0:2048].rearrange("p (c d) -> p c d", c=DC)
            for i in range(4):
                cols = slice(512 * i, 512 * (i + 1))
                wait(dve, tern_f, i)
                V.tensor_scalar(below, wf_st[:, :, cols], theta[:, 0, 1:2], None, ALU.is_lt
                                ).then_inc(below_done, 1)
                dve.wait_ge(below_done, 2 + i + 1)
                V.scalar_tensor_tensor(wf[:, :, cols], wf_st[:, :, cols], theta[:, 0, 0:1], below,
                                       ALU.is_gt, ALU.subtract).then_inc(tern_f, 1)
            for c in (0, 2):
                dve.wait_ge(s_wp[c], 16)
                V.tensor_reduce(absum[:, 1, c:c + 1], wp_st[c // 2][:, 4 * (c % 2):4 * (c % 2) + 4, :], AX.XY,
                                ALU.add, apply_absolute_value=True).then_inc(abs_dve, 1)
            dve.wait_ge(scal, 5)
            V.tensor_scalar(cs[:], gam[:, 0:1], 0.5 / 64, None, ALU.mult).then_inc(scal, 1)

            def first(b):
                if b == 0:
                    dve.wait_ge(total_ready, 2)
                    V.tensor_reduce(gam[:, 1:2], A[0][:, 0:4], AX.X, ALU.add).then_inc(scal, 1)
                    dve.wait_ge(scal, 7)
                    V.tensor_scalar(gam[:, 1:2], gam[:, 1:2], 1.0 / (D * F), None, ALU.mult).then_inc(scal, 1)
                    dve.wait_ge(scal, 8)
                    V.tensor_scalar(theta[:, 1, 0:1], gam[:, 1:2], EPS_BIT, 0.5, ALU.add, ALU.mult
                                    ).then_inc(thr_p, 1)
                    V.tensor_scalar(theta[:, 1, 1:2], gam[:, 1:2], EPS_BIT, -0.5, ALU.add, ALU.mult
                                    ).then_inc(thr_p, 1)
                    dve.wait_ge(scal, 6)
                    V.tensor_tensor(cs[:], cs[:], gam[:, 1:2], ALU.mult).then_inc(thr_p, 1)
                    dve.wait_ge(thr_p, 3)
                if b < 4:
                    i = b
                    src = wp_st[i // 2][:, 4 * (i % 2):4 * (i % 2) + 4, :]
                    lowv = low16[:]
                    wait(dve, tern_p, i)
                    V.tensor_scalar(lowv, src, theta[:, 1, 1:2], None, ALU.is_lt).then_inc(thr_p, 1)
                    dve.wait_ge(thr_p, 3 + i + 1)
                    V.scalar_tensor_tensor(wp[:, 4 * i:4 * i + 4, :], src, theta[:, 1, 0:1], lowv,
                                           ALU.is_gt, ALU.subtract).then_inc(tern_p, 1)
                if b == 4:
                    dve.wait_ge(s_WT, 16)
                    dve.wait_ge(s_b, 16)
                    V.tensor_reduce(acol[:], WT_st, AX.X, ALU.max, apply_absolute_value=True
                                    ).then_inc(ub_chain, 1)
                    V.tensor_reduce(babs[:], bcol[:, 0:8].rearrange("p (c a) -> p c a", a=1), AX.X, ALU.max,
                                    apply_absolute_value=True).then_inc(ub_chain, 1)
                    dve.wait_ge(ub_chain, 2)
                    V.tensor_tensor(acol[:], acol[:], babs[:], ALU.max).then_inc(ub_chain, 1)
                    dve.wait_ge(ub_chain, 3)
                    V.reciprocal(ra[:], acol[:]).then_inc(ub_chain, 1)
                    dve.wait_ge(ub_chain, 4)
                    V.tensor_scalar(raS[:], ra[:], US, None, ALU.mult).then_inc(ub_chain, 1)
                    V.tensor_tensor(bn[:], bcol[:, 0:8], ra[:], ALU.mult).then_inc(ub_chain, 1)
                    dve.wait_ge(ub_chain, 6)
                if b == 5:
                    for j in range(2):
                        for c in range(DC):
                            last = V.tensor_scalar(diag[:, j, c, :], id32[:], raS[:, 4 * j + c:4 * j + c + 1], None,
                                                   ALU.mult)
                        last.then_inc(ub_diag, 1)
                if 7 <= b < 11:
                    if b == 7:
                        dve.wait_ge(s_W, 16)
                    for i in (2 * (b - 7), 2 * (b - 7) + 1):
                        j, c = i // 4, i % 4
                        dve.wait_ge(ub_row, j + 1)
                        if i >= 2:
                            dve.wait_ge(ub_lo, i - 1)
                        V.tensor_tensor(ub[:, i % 2, :], S[j][:], W_st[:, c, j, :], ALU.mult
                                        ).then_inc(ub_prod, 1)
            def first_all(b):
                first_low(b)
                first(b)
                if b == 12:
                    dve.wait_ge(tsum_ready, 1)
                    V.tensor_copy(Tsum[:], S[1][:]).then_inc(tsum_saved, 1)

            def first_low(b):
                if 8 <= b < 12:
                    for i in (2 * (b - 8), 2 * (b - 8) + 1):
                        dve.wait_ge(ub_hi, i + 1)
                        V.tensor_tensor(U[:, i // 4, 1, i % 4, :], ub[:, i % 2, :], U[:, i // 4, 0, i % 4, :],
                                        ALU.subtract).then_inc(ub_lo, 1)

            dve.wait_ge(s_x[1], 16)
            tile(0, False, False, True, first_all, post=False)
            for t in range(2, NT):
                dve.wait_ge(s_x[t], 16)
            dve.wait_ge(g_zero, 2)
            dve.wait_ge(tsum_saved, 1)
            with dve.Fori(1, TPB + 1) as n:
                tile(n, True, False, True)

            def quad(o, n):
                dve.wait_ge(gram_saved, DC * TPB * (o + 1))
                for m in range(DC):
                    V.tensor_copy(GH[:, 0, m, m * P:D], Gacc[:, m, m * P:D]).then_inc(g_hi, 1)
                for m in range(DC):
                    dve.wait_ge(g_hi, DC * o + m + 1)
                    V.tensor_tensor(GH[:, 1, m, m * P:D], Gacc[:, m, m * P:D], GH[:, 0, m, m * P:D],
                                    ALU.subtract).then_inc(g_lo, 1)
                dve.wait_ge(gt_ready, 2 * (o + 1))
                k = 0
                for i in range(DC - 1):
                    w = DC - 1 - i
                    last = V.tensor_copy(GH[:, 1, i + 1:DC, i * P:(i + 1) * P],
                                         S[1][:].bitcast(F16)[:, k * P:(k + w) * P].rearrange("p (c d) -> p c d", c=w))
                    k += w
                last.then_inc(gt_saved, 1)
                post_rows(n, n % NT)
                post_product(n, n % NT, 1)
                for g in range(DC):
                    m = DC - 1 - g
                    r = 2 if g % 2 == 0 else 0
                    dve.wait_ge(s_wst[g % 2], 16 * (2 * o + g // 2 + 1))
                    wq_, wk_, wv_ = (Wst[g % 2][:, j, :] for j in range(3))
                    dve.wait_ge(gu_ready, 2 * (DC * o + g) + 1)
                    if g == 0:
                        V.tensor_tensor(sums[:, 0, :], QB[r][:], wk_, ALU.mult).then_inc(qd, 1)
                        V.tensor_tensor(sums[:, 1, :], QB[r][:], wv_, ALU.mult).then_inc(gu_saved, 1)
                        dve.wait_ge(gu_ready, 2 * (DC * o + g) + 2)
                        V.tensor_tensor(sums[:, 2, :], QB[r + 1][:], wq_, ALU.mult).then_inc(gu_saved, 1)
                    else:
                        dve.wait_ge(qd, QN * o + 3 * g - 2)
                        V.tensor_tensor(term[0], QB[r][:], wk_, ALU.mult).then_inc(qt, 1)
                        V.tensor_tensor(term[1], QB[r][:], wv_, ALU.mult).then_inc(gu_saved, 1)
                        dve.wait_ge(qt, (DC - 1) * o + g)
                        V.tensor_tensor(sums[:, 0, :], sums[:, 0, :], term[0], ALU.add).then_inc(qd, 1)
                        dve.wait_ge(gu_ready, 2 * (DC * o + g) + 2)
                        V.tensor_tensor(term[2], QB[r + 1][:], wq_, ALU.mult).then_inc(gu_saved, 1)
                        dve.wait_ge(gu_saved, 2 * (DC * o + g) + 1)
                        V.tensor_tensor(sums[:, 1, :], sums[:, 1, :], term[1], ALU.add).then_inc(qd, 1)
                        dve.wait_ge(gu_saved, 2 * (DC * o + g) + 2)
                        V.tensor_tensor(sums[:, 2, :], sums[:, 2, :], term[2], ALU.add).then_inc(qd, 1)
                dve.wait_ge(mw_ready, 3 * (DC - 1) * (o + 1))
                V.memset(mu[:], 0.0).then_inc(g_zero, 1)
                V.memset(Gacc[:], 0.0).then_inc(g_zero, 1)
                dve.wait_ge(g_zero, 2 * (o + 2))
                dve.wait_ge(red_ready, o + 1)
                V.tensor_copy(red[:], H[0][:, 0:6 * DC]).then_inc(red_saved, 1)

            def quad_scale(o):
                def chain(ins):
                    c0[0] += 1
                    ins.then_inc(red_chain, 1)
                    dve.wait_ge(red_chain, c0[0])

                def chain_v(ins):
                    c1[0] += 1
                    ins.then_inc(sc_chain, 1)
                    dve.wait_ge(sc_chain, c1[0])

                c0, c1 = [RC * o], [5 * o]
                dve.wait_ge(red_saved, o + 1)
                kk_, kv_, qq_, mk, mv, mq = (red[:, DC * i:DC * (i + 1)] for i in range(6))
                bq, bk, bv = (bcol[:, DC * i:DC * (i + 1)] for i in range(3))
                n_q, n_k = bn[:, 0:DC], bn[:, DC:2 * DC]
                r_q, r_k = ra[:, 0:DC], ra[:, DC:2 * DC]
                chain(V.tensor_tensor(mk, mk, r_k, ALU.mult))
                chain(V.scalar_tensor_tensor(k1[:], n_k, float(T * TS), mk, ALU.mult, ALU.add))
                chain(V.tensor_tensor(mq, mq, r_q, ALU.mult))
                chain(V.scalar_tensor_tensor(q1[:], n_q, float(T * TS), mq, ALU.mult, ALU.add))
                chain(V.tensor_tensor(kk[:], bk, mk, ALU.mult))
                chain(V.tensor_tensor(kk[:], kk[:], kk_, ALU.add))
                chain(V.tensor_tensor(qq[:], bq, mq, ALU.mult))
                chain(V.tensor_tensor(qq[:], qq[:], qq_, ALU.add))
                chain(V.tensor_tensor(k2[:], bk, k1[:], ALU.mult))
                chain(V.tensor_tensor(kk[:], kk[:], k2[:], ALU.add))
                chain(V.tensor_tensor(q2[:], bq, q1[:], ALU.mult))
                chain(V.tensor_tensor(qq[:], qq[:], q2[:], ALU.add))
                chain(V.tensor_tensor(kk[:], kk[:], r_k, ALU.mult))
                chain(V.tensor_tensor(qq[:], qq[:], r_q, ALU.mult))
                chain(V.tensor_tensor(prod[:], kk[:], qq[:], ALU.mult))
                chain_v(V.tensor_tensor(kv[:], bv, k1[:], ALU.mult))
                chain_v(V.tensor_tensor(kv[:], kv[:], kv_, ALU.add))
                chain_v(V.tensor_tensor(k2[:], n_k, mv, ALU.mult))
                chain_v(V.tensor_tensor(kv[:], kv[:], k2[:], ALU.add))
                dve.wait_ge(s_pow, o + 1)
                chain_v(V.tensor_tensor(sc2[:], kv[:], ip[:], ALU.mult))
                V.tensor_scalar(scol[:], sc2[:], 1.0 / (XS * US), None, ALU.mult).then_inc(sc_one, 1)
                V.tensor_tensor(bsc[:], sc2[:], n_q, ALU.mult).then_inc(sc_one, 1)
                dve.wait_ge(sc_one, 2 * (o + 1))
                for j, col in ((0, scol), (1, bsc)):
                    for c in range(DC):
                        last = V.tensor_scalar(diag[:, j, c, :], id32[:], col[:, c:c + 1], None, ALU.mult)
                    last.then_inc(s_diag, 1)

            def quad_rows(o):
                for j, row in ((0, Srow), (1, Brow)):
                    dve.wait_ge(s_row, 2 * o + j + 1)
                    V.tensor_copy(row[:], S[j][:]).then_inc(s_saved, 1)
                dve.wait_ge(s_saved, 2 * (o + 1))

            quad(0, TPB)
            quad_scale(0)
            tile(TPB + 1, True, False, True, post=False)
            for n in range(TPB + 2, NT - 1):
                tile(n, True, False, True)
            ln_lows("Q", 0, 0, hlQ)
            ln_lows("Q", 0, 1, hlQ)
            quad_rows(0)
            with dve.Fori(NT - 1, NT + 1) as n:
                tile(n, True, True, True)
            quad(1, NT)
            quad_scale(1)
            tile(NT + 1, False, True, True, post=False)
            tile(NT + 2, False, True, True)
            quad_rows(1)
            with dve.Fori(NT + 3, 2 * NT - 2) as n:
                tile(n, False, True, True)
            tile(2 * NT - 2, False, True, True, next_q=False)
            tile(2 * NT - 1, False, False, False)
            post_rows(2 * NT - 1, NT - 1)
            post_product(2 * NT - 1, NT - 1, 1)


def kernel(L0_attn_x, L0_attn_W, L0_attn_b, L0_ffn_w_fc, L0_ffn_w_proj):
    import numpy as np
    import concourse.bacc as bacc
    from concourse.bass_utils import run_bass_kernel_spmd as run

    nc = bacc.Bacc("TRN2", target_bir_lowering=False, num_devices=1)
    arrays = {
        "x": np.ascontiguousarray(L0_attn_x),
        "WT": np.ascontiguousarray(np.transpose(L0_attn_W)),
        "W": np.ascontiguousarray(L0_attn_W),
        "b": np.ascontiguousarray(L0_attn_b),
        "wfT": np.ascontiguousarray(np.transpose(L0_ffn_w_fc)),
        "wpT": np.ascontiguousarray(np.transpose(L0_ffn_w_proj)),
    }
    args = [nc.dram_tensor(n, a.shape, F32, kind="ExternalInput").ap() for n, a in arrays.items()]
    out = nc.dram_tensor("out", arrays["x"].shape, F32, kind="ExternalOutput").ap()
    macaron_kernel(nc, *args, out)
    return run(nc, [arrays], core_ids=[0]).results[0]["out"]
```

```python
from contextlib import ExitStack

import concourse.bass as bass
from concourse import mybir

F32 = mybir.dt.float32
F16 = mybir.dt.float16
ALU = mybir.AluOpType
ACT = mybir.ActivationFunctionType
AX = mybir.AxisListType

P = 128
EPS_LN = 1e-5
EPS_BIT = 1e-6
XS = 2048.0
US = 1024.0
GS = 2.0 ** -5
AS1 = 2.0 ** -4
AS2 = 2.0 ** -19
TS = GS * US


def wait(eng, sem, value):
    if isinstance(value, int) and value <= 0:
        return
    eng.wait_ge(sem, value)


def macaron_kernel(nc, x, WT, W, b, wfT, wpT, out):
    NB, T, D = x.shape
    F = wfT.shape[1]
    DC = D // P
    FB = F // P
    SUB = 4
    TOK = SUB * P
    NT = NB * T // TOK
    TPB = T // TOK
    RING = 4
    LAG = 4
    STEPS = FB
    NS = NT * SUB

    x_v = x.rearrange("b (s p) d -> p (b s) d", p=P)
    out_v = out.rearrange("b (s p) d -> p (b s) d", p=P)
    wf_v = wfT.rearrange("(c p) f -> p c f", p=P)
    wp_v = wpT.rearrange("(c p) o -> p c o", p=P)
    WT_v = WT.rearrange("(c p) d -> p c d", p=P)
    W_v = W.rearrange("(c p) n -> p c n", p=P)
    b_v = b.rearrange("(c p) -> p c", p=P)

    with ExitStack() as ctx:
        def sb(name, shape, dt=F32):
            return ctx.enter_context(nc.sbuf_tensor(name, shape, dt))

        def sem(name):
            return ctx.enter_context(nc.semaphore(name))

        X = sb("X", [P, NS, D])
        wf = sb("wf", [P, DC, F], F16)
        wp = sb("wp", [P, FB, D], F16)
        xT = sb("xT", [P, 2, DC, TOK], F16)
        qT = sb("qT", [P, 2, 2, DC, P], F16)
        G2 = sb("G2", [P, LAG, 2, TOK], F16)
        U = sb("U", [P, 2, 2, DC, D], F16)
        sq = sb("sq", [P, RING, TOK])
        Gacc = sb("Gacc", [P, DC, D])
        acc1 = sb("acc1", [P, TOK])
        acc2 = sb("acc2", [P, TOK])
        Tsum = sb("Tsum", [P, D])
        SB = sb("SB", [P, 2, D])
        Srow, Brow = SB[:, 0, :], SB[:, 1, :]
        ones32 = sb("ones32", [P, P])
        ones16 = sb("ones16", [P, P], F16)
        id32 = sb("id32", [P, P])
        id16 = sb("id16", [P, P], F16)
        scratch = sb("scratch", [P, 10240])

        def region(a, n, dt=F32):
            r = scratch[:, a:a + n]
            return r.bitcast(dt) if dt != F32 else r

        hl = region(0, 2048, F16).rearrange("p (h s d) -> p h s d", h=2, s=SUB)
        hlA = region(2048, 2048, F16).rearrange("p (h s d) -> p h s d", h=2, s=SUB)
        hlQ = region(4096, 2048, F16).rearrange("p (h s d) -> p h s d", h=2, s=SUB)
        gf = region(6144, 2048).rearrange("p (r t) -> p r t", r=4)
        accp = region(6144, 1024, F16).rearrange("p (a h t) -> p a h t", a=2, h=2)
        vb = region(8192, 1024).rearrange("p (r t) -> p r t", r=2)
        ub = region(9216, 1024).rearrange("p (r t) -> p r t", r=2)
        sums = G2[:].rearrange("p a h t -> p (a h t)").bitcast(F32).rearrange("p (r t) -> p r t", r=4)
        more = region(8192, 1024).rearrange("p (r t) -> p r t", r=2)
        mu_sum = [sums[:, 3, :], more[:, 0, :], more[:, 1, :]]
        qT32 = qT[:].rearrange("p a h c t -> p (a h c t)").bitcast(F32)
        mu_term = [qT32[:, 0:512], qT32[:, 512:1024], region(9728, 512)]
        Wst = [region(a, 1536).rearrange("p (j d) -> p j d", j=3) for a in (2048, 0)]
        GH = region(6144, 2048, F16).rearrange("p (h c d) -> p h c d", h=2, c=DC)
        term = [region(a, 512) for a in (3584, 1536, 9216)]
        low16 = SB[:].rearrange("p j d -> p (j d)").bitcast(F16).rearrange("p (s d) -> p s d", d=D)
        wf_st = X[:, 4 * SUB:8 * SUB, :].rearrange("p (c s) d -> p c (s d)", c=DC)
        wp_st = [X[:, 2 * SUB:4 * SUB, :], region(2048, 4096).rearrange("p (c d) -> p c d", d=D)]
        WT_st = X[:, 4 * SUB:6 * SUB, :]
        ut = region(4096, 2048, F16).rearrange("p (r h d) -> p r h d", r=4, h=2)

        def small(name, *shape):
            return sb(name, [P, *shape])

        st = small("st", SUB, 6)
        stA = small("stA", SUB, 6)
        mF, msum, mdif, vsum, vdif, vtot = (small(n, SUB) for n in ("mF", "msum", "mdif", "vsum", "vdif", "vtot"))
        mA, nbF = small("mA", SUB), small("nbF", SUB)
        ve, pw, rz, zz, rf = (small(n, SUB) for n in ("ve", "pw", "rz", "zz", "rf"))
        veA, pwA = small("veA", SUB), small("pwA", SUB)
        rA, nbA = small("rA", NS), small("nbA", NS)
        negmk, nmc, m2, var, varc, veP, pwP, rzP, zP, cP = (
            small(n, SUB) for n in ("negmk", "nmc", "m2", "var", "varc", "veP", "pwP", "rzP", "zP", "cP"))
        half = small("half", SUB)
        absum = small("absum", 2, 5)
        warm = small("warm", 1)
        gam = small("gam", 2)
        theta = small("theta", 2, 2)
        hscale, kap, cs, kinv, kacc1, kacc2, ksq = (
            small(n, 1) for n in ("hscale", "kap", "cs", "kinv", "kacc1", "kacc2", "ksq"))
        mu = small("mu", DC)
        bcol = small("bcol", 12)
        acol, babs, ra, bn, raS = (small(n, 8) for n in ("acol", "babs", "ra", "bn", "raS"))
        red = small("red", 24)
        k1, q1, k2, q2, kk, qq, kv, prod, ip, scol, bsc, sc2 = (
            small(n, DC) for n in ("k1", "q1", "k2", "q2", "kk", "qq", "kv", "prod", "ip", "scol", "bsc", "sc2"))
        diag = sb("diag", [P, 2, 4, P])

        def bank(name):
            return ctx.enter_context(nc.psum_tensor(name, [P, 512], F32))

        H = [bank("H0"), bank("H1")]
        A = [bank(f"A{s}") for s in range(SUB)]
        S = [bank("S0"), bank("S1")]

        QB = S + H

        s_x = [sem(f"x_loaded{t}") for t in range(NT)]
        s_wf = [sem(f"wf_loaded{c}") for c in range(DC)]
        s_wp = [sem(f"wp_loaded{c}") for c in range(4)]
        s_WT, s_b = sem("WT_loaded"), sem("b_loaded")
        s_wst = [sem("Wchunk_loaded0"), sem("Wchunk_loaded1")]
        out_stored = sem("out_stored")
        const_ready = sem("const_ready")
        abs_dve, abs_act = sem("abs_dve"), sem("abs_act")
        total_ready = sem("total_ready")
        scal = sem("scalars_chain")
        thr_f = sem("thr_f")
        low_ready = sem("mask_ready")
        tern_f, tern_p = sem("tern_f"), sem("tern_p")
        tsum_ready, tsum_saved = sem("tsum_ready"), sem("tsum_saved")
        u_chain, u_scale, u_hi, u_lo, u_ready = (
            sem(n) for n in ("u_chain", "u_scale", "u_hi", "u_lo", "u_transposed"))
        u_saved = [sem("u_saved0"), sem("u_saved1")]
        ln_stat, ln_aggr, ln_pre, ln_pow, ln_r, ln_v, ln_hi, ln_lo = (
            {k: sem(f"{n}{k}") for k in "FAQ"} for n in
            ("ln_stat", "ln_aggr", "ln_pre", "ln_pow", "ln_r", "ln_v", "ln_hi", "ln_lo"))
        ln_mean = {k: sem(f"ln_mean{k}") for k in "FA"}
        t_ready, t_saved = sem("t_ready"), sem("t_saved")
        h_ready, gelu_done, sq_done, hi_done, lo_done, acc_done, acc_one, proj_done = (
            sem(n) for n in ("h_ready", "gelu_done", "sq_done", "hi_done", "lo_done", "acc_done",
                             "acc_one", "proj_done"))
        acc_hi, acc_lo, k_ready = sem("acc_hi"), sem("acc_lo"), sem("k_ready")
        stat_ready, post_step, post_pre, post_pow, p_sub, x_pre, x_sub = (
            sem(n) for n in ("stat_ready", "post_step", "post_pre", "post_pow", "p_sub", "x_pre", "x_sub"))
        gram_ready, gram_saved = sem("gram_ready"), sem("gram_saved")
        mu_saved = sem("mu_saved")
        qt_ready, qt_saved, q_ready, q_mul, q_add, q_saved = (
            sem(n) for n in ("qt_ready", "qt_saved", "q_ready", "q_mul", "q_add", "q_saved"))
        g_hi, g_lo, g_zero, gt_ready, gt_saved = (sem(n) for n in ("g_hi", "g_lo", "g_zero", "gt_ready", "gt_saved"))
        gu_ready, gu_saved, qd, red_ready, red_chain, s_pow, s_diag, s_row, s_saved = (
            sem(n) for n in ("gu_ready", "gu_saved", "quad_chain", "red_ready", "red_chain",
                             "s_pow", "s_diag", "s_row", "s_saved"))

        mw_prod, mw_ready = sem("mu_W_product"), sem("mu_W_sum")
        qt, red_saved = sem("quad_term"), sem("red_saved")
        thr_p, sc_chain, sc_one = sem("thr_p"), sem("sc_chain"), sem("sc_one")

        POST = 8
        QN = 1 + 3 * (DC - 1)
        RC = 15

        block = ctx.enter_context(nc.Block())

        @block.sync
        def _(sp):
            def load_x(t):
                sp.dma_start(X[:, t * SUB:(t + 1) * SUB, :],
                             x_v[:, t * SUB:(t + 1) * SUB, :]).then_inc(s_x[t], 16)

            load_x(0)
            for c in range(DC):
                sp.dma_start(wf_st[:, c, :], wf_v[:, c, :]).then_inc(s_wf[c], 16)
            for c in range(4):
                sp.dma_start(wp_st[c // 2][:, 4 * (c % 2):4 * (c % 2) + 4, :],
                             wp_v[:, 4 * c:4 * c + 4, :]).then_inc(s_wp[c], 16)
            with nc.allow_non_contiguous_dma(reason="the bias, one element per partition"):
                sp.dma_start(bcol[:], b_v).then_inc(s_b, 16)
            load_x(1)
            sp.wait_ge(tern_f, 5)
            sp.dma_start(WT_st, WT_v[:, 0:8, :]).then_inc(s_WT, 16)
            load_x(6)
            load_x(7)
            sp.wait_ge(tern_p, 4)
            load_x(2)
            load_x(3)
            sp.wait_ge(u_lo, 8)
            load_x(4)
            load_x(5)
            for o in range(NB):
                for c in range(DC):
                    if c == 0:
                        sp.wait_ge(gram_ready, DC * TPB * (o + 1))
                    if c == 1:
                        sp.wait_ge(t_ready, SUB * (TPB * (o + 1) + 2))
                    if c >= 2:
                        sp.wait_ge(gu_saved, 2 * (DC * o + c - 1))
                        sp.wait_ge(mw_prod, 3 * (DC * o + c - 1))
                    sp.dma_start(Wst[c % 2], W_v[:, DC - 1 - c, :].rearrange("p (j d) -> p j d", j=3)
                                 ).then_inc(s_wst[c % 2], 16)
            with sp.Fori(0, NT - 1) as m:
                sp.wait_ge(x_sub, SUB * (m + NT + 1))
                sp.dma_start(out_v[:, bass.ts(m, SUB), :], X[:, bass.ts(m, SUB), :]).then_inc(out_stored, 16)
            for s in range(SUB):
                r = (NT - 1) * SUB + s
                sp.wait_ge(x_sub, SUB * (2 * NT - 1) + s + 1)
                sp.dma_start(out_v[:, r, :], X[:, r, :]).then_inc(out_stored, 16)
            sp.wait_ge(out_stored, 16 * (NT - 1 + SUB))

        @block.gpsimd
        def _(pool):
            nc.gpsimd.memset(half[:], -0.5).then_inc(const_ready, 1)
            nc.gpsimd.memset(ones32[:], 1.0).then_inc(const_ready, 1)
            nc.gpsimd.memset(ones16[:], 1.0).then_inc(const_ready, 1)
            nc.gpsimd.memset(id32[:], 0.0).then_inc(const_ready, 1)
            nc.gpsimd.memset(id16[:], 0.0).then_inc(const_ready, 1)
            pool.wait_ge(const_ready, 5)
            for m in (id32, id16):
                nc.gpsimd.affine_select(out=m[:], in_=m[:], compare_op=ALU.not_equal, fill=1.0, base=0,
                                        pattern=[[-1, P]], channel_multiplier=1).then_inc(const_ready, 1)

            def rsqrt(dst, src, pre, done, k, per=1):
                pool.wait_ge(pre, per * (k + 1))
                nc.gpsimd.tensor_tensor(dst[:], src[:], half[:], ALU.pow).then_inc(done, 1)

            def tile(n, gram, nxt, with_q=False):
                for b in range(STEPS):
                    if b:
                        pool.wait_ge(gelu_done, FB * n + b + 1)
                        if b > 1:
                            pool.wait_ge(acc_one, (FB - 1) * n + b - 1)
                        nc.gpsimd.tensor_tensor(acc1[:], acc1[:] if b > 1 else gf[:, 0, :], gf[:, b % RING, :],
                                                ALU.add).then_inc(acc_one, 1)
                    if gram and b == 1:
                        rsqrt(pwA, veA, ln_pre["A"], ln_pow["A"], n - 1)
                    if nxt and b == (9 if with_q else 8):
                        rsqrt(pw, ve, ln_pre["F"], ln_pow["F"], n + 1)
                rsqrt(pwP, veP, post_pre, post_pow, n)

            def quad(o):
                for g in range(1, DC):
                    for i in range(3):
                        pool.wait_ge(mw_prod, 3 * (DC * o + g) + i + 1)
                        if g > 1:
                            pool.wait_ge(mw_ready, 3 * ((DC - 1) * o + g - 2) + i + 1)
                        nc.gpsimd.tensor_tensor(mu_sum[i], mu_sum[i], mu_term[i], ALU.add).then_inc(mw_ready, 1)

            rsqrt(pw, ve, ln_pre["F"], ln_pow["F"], 0)
            tile(0, False, True)
            with pool.Fori(1, TPB + 1) as n:
                tile(n, True, True)
            quad(0)
            rsqrt(ip, prod, red_chain, s_pow, 0, RC)
            with pool.Fori(TPB + 1, NT - 1) as n:
                tile(n, True, True)
            with pool.Fori(NT - 1, NT + 1) as n:
                tile(n, True, True, True)
            quad(1)
            rsqrt(ip, prod, red_chain, s_pow, 1, RC)
            with pool.Fori(NT + 1, NT + 3) as n:
                tile(n, False, True, True)
            with pool.Fori(NT + 3, 2 * NT - 1) as n:
                tile(n, False, True, True)
            tile(2 * NT - 1, False, False)

        @block.tensor
        def _(pe):
            def transposes(i, k, src, sm_lo, dst_bank, done, chunk=0):
                ps = dst_bank[:].bitcast(F16).rearrange("p (h c t) -> p h c t", h=2, c=DC)
                pe.wait_ge(sm_lo, SUB * k + i + 1)
                for h in range(2):
                    for c in range(DC):
                        last = nc.tensor.transpose(ps[:, h, c, :], src[:, h, i, c * P:(c + 1) * P], id16[:])
                last.then_inc(done, 1)

            def fc(n, b):
                B = FB * n + b
                wait(pe, gelu_done, B - 1)
                for c in range(DC):
                    for h in range(2):
                        last = nc.tensor.matmul(H[b % 2][:], wf[:, c, b * P:(b + 1) * P], xT[:, h, c, :],
                                                start=(c == 0 and h == 0), stop=(c == DC - 1 and h == 1))
                last.then_inc(h_ready, 1)

            def proj(n, b):
                pe.wait_ge(lo_done, FB * n + b + 1)
                if b == 0:
                    wait(pe, x_sub, SUB * n)
                for s in range(SUB):
                    for h in range(2):
                        last = nc.tensor.matmul(A[s][:], G2[:, b % LAG, h, s * P:(s + 1) * P], wp[:, b, :],
                                                start=(b == 0 and h == 0), stop=(b == FB - 1 and h == 1))
                    if b == FB - 1:
                        last.then_inc(p_sub, 1)
                if b < FB - 1:
                    last.then_inc(proj_done, 1)

            def gram(n, m, with_q):
                if m == 0:
                    pe.wait_ge(ln_lo["A"], SUB * n)
                if m < 2 and with_q:
                    pe.wait_ge(q_mul, SUB * (n - (NT - 1)) + 3 + m)
                if m >= 2:
                    pe.wait_ge(gram_saved, DC * (n - 1) + m - 1)
                w = D - m * P
                g = S[m % 2]
                for s in range(SUB):
                    for i, (l, r) in enumerate(((0, 0), (0, 1), (1, 0))):
                        last = nc.tensor.matmul(g[:, 0:w], hlA[:, l, s, m * P:(m + 1) * P],
                                                hlA[:, r, s, m * P:D],
                                                start=(s == 0 and i == 0), stop=(s == SUB - 1 and i == 2))
                if m == DC - 1:
                    for c in range(DC):
                        for s in range(SUB):
                            for h in range(2):
                                last = nc.tensor.matmul(g[:, 256 + c:257 + c], hlA[:, h, s, c * P:(c + 1) * P],
                                                        ones16[:, 0:1], start=(s == 0 and h == 0),
                                                        stop=(s == SUB - 1 and h == 1))
                last.then_inc(gram_ready, 1)

            def q_transpose(n, s):
                m = n - (NT - 1)
                if s >= 2:
                    pe.wait_ge(q_mul, SUB * m + s - 1)
                transposes(s, m, hlQ, ln_lo["Q"], S[s % 2], qt_ready)

            def q_product(n, s):
                m = n - (NT - 1)
                pe.wait_ge(qt_saved, SUB * m + s + 1)
                for c in range(DC):
                    for i, (l, r) in enumerate(((0, 0), (0, 1), (1, 0))):
                        last = nc.tensor.matmul(S[s % 2][:], qT[:, s % 2, l, c, :], U[:, 0, r, c, :],
                                                start=(c == 0 and i == 0), stop=(c == DC - 1 and i == 2))
                last.then_inc(q_ready, 1)

            def tile(n, with_gram, with_q, nxt, hooks=None):
                if with_q:
                    pe.wait_ge(post_step, POST * (n - 1) + 3)
                    q_transpose(n, 0)
                    pe.wait_ge(t_saved, SUB * n + 2)
                    q_transpose(n, 1)
                for b in range(LAG):
                    if b == 0:
                        pe.wait_ge(t_saved, SUB * (n + 1))
                    if hooks:
                        hooks(b)
                    fc(n, b)
                    if with_q and b in (1, 2):
                        q_product(n, b - 1)
                for b in range(LAG, STEPS):
                    if hooks:
                        hooks(b)
                    fc(n, b)
                    if hooks and (b - LAG) % 4 == 0:
                        pe.wait_ge(tern_p, (b - LAG) // 4 + 1)
                    proj(n, b - LAG)
                    if with_q:
                        if b in (5, 6):
                            q_transpose(n, b - 3)
                        if b in (7, 8):
                            q_product(n, b - 5)
                    if with_gram and 10 <= b < 14:
                        if hooks and b == 10:
                            pe.wait_ge(u_saved[0], 2 * n)
                            pe.wait_ge(u_saved[1], 2 * n)
                        gram(n, b - 10, with_q)
                for i in range(SUB):
                    if hooks and i == 0:
                        pe.wait_ge(tern_p, 4)
                    if i == 3:
                        stats(n, nxt)
                    proj(n, FB - LAG + i)
                    if nxt and i < 2:
                        if i == 0:
                            if with_gram:
                                pe.wait_ge(gram_saved, DC * n)
                            if with_q:
                                pe.wait_ge(q_mul, SUB * (n - (NT - 2)))
                            if hooks:
                                pe.wait_ge(tsum_saved, 1)
                        else:
                            pe.wait_ge(gelu_done, FB * (n + 1))
                        for j in (2 * i, 2 * i + 1):
                            transposes(j, n + 1, hl, ln_lo["F"], QB[j], t_ready)

            def stats(n, nxt):
                pe.wait_ge(acc_lo, 2 * (n + 1))
                if nxt:
                    pe.wait_ge(t_saved, SUB * (n + 1) + 1)
                for j in range(2):
                    for s in range(SUB):
                        for h in range(2):
                            last = nc.tensor.matmul(S[0][:, SUB * j + s:SUB * j + s + 1],
                                                    accp[:, j, h, s * P:(s + 1) * P], ones16[:, 0:1],
                                                    start=(h == 0), stop=(h == 1))
                last.then_inc(stat_ready, 1)

            def quad(o, n):
                pe.wait_ge(g_lo, DC * (o + 1))
                pe.wait_ge(t_saved, SUB * (n + 2))
                pe.wait_ge(post_step, POST * n + 3)
                for h in range(2):
                    ps = S[h][:].bitcast(F16)
                    k = 0
                    for i in range(DC - 1):
                        for j in range(i + 1, DC):
                            last = nc.tensor.transpose(ps[:, k * P:(k + 1) * P], GH[:, h, i, j * P:(j + 1) * P],
                                                       id16[:])
                            k += 1
                    last.then_inc(gt_ready, 1)
                for g in range(DC):
                    m = DC - 1 - g
                    if g == 1:
                        pe.wait_ge(gt_saved, 2 * (o + 1))
                    for j, r in ((1, 0), (0, 1)):
                        r += 2 if g % 2 == 0 else 0
                        if g >= 2:
                            pe.wait_ge(gu_saved, 2 * (DC * o + g - 2) + r % 2 + 1)
                        for c in reversed(range(DC)) if g else range(DC):
                            first_c = DC - 1 if g else 0
                            last_c = DC - 1 - first_c
                            for i, (l, h) in enumerate(((0, 0), (0, 1), (1, 0))):
                                last = nc.tensor.matmul(QB[r][:], GH[:, l, c, m * P:(m + 1) * P], U[:, j, h, c, :],
                                                        start=(c == first_c and i == 0),
                                                        stop=(c == last_c and i == 2))
                        last.then_inc(gu_ready, 1)
                for r in (3, 4, 5, 0, 1, 2):
                    if r == 3:
                        pe.wait_ge(gu_saved, 2 * (DC * o + 2) + 2)
                        pe.wait_ge(mw_ready, 3 * (DC - 1) * (o + 1))
                    if r == 0:
                        pe.wait_ge(qd, QN * (o + 1))
                    a = sums[:, r, :] if r < 4 else more[:, r - 4, :]
                    for c in range(DC):
                        last = nc.tensor.matmul(H[0][:, DC * r + c:DC * r + c + 1], a[:, c * P:(c + 1) * P],
                                                ones32[:, 0:1], start=True, stop=True)
                last.then_inc(red_ready, 1)
                pe.wait_ge(red_saved, o + 1)

            def rows(o, n):
                pe.wait_ge(t_saved, SUB * (n + 2))
                pe.wait_ge(post_step, POST * n + 3)
                for j in range(2):
                    pe.wait_ge(s_diag, 2 * o + j + 1)
                    for c in range(DC):
                        last = nc.tensor.matmul(S[j][:, c * P:(c + 1) * P], ones32[:], diag[:, j, c, :],
                                                start=True, stop=True)
                    last.then_inc(s_row, 1)
                pe.wait_ge(s_saved, 2 * (o + 1))

            pe.wait_ge(const_ready, 7)
            for i in range(SUB):
                transposes(i, 0, hl, ln_lo["F"], QB[i], t_ready)
            pe.wait_ge(abs_dve, 3)
            pe.wait_ge(abs_act, 2)
            nc.tensor.matmul(A[1][:, 0:5], ones32[:], absum[:, 0, :], start=True, stop=True
                             ).then_inc(total_ready, 1)

            def first(b):
                if b < 2 or b % 4 == 0:
                    pe.wait_ge(tern_f, b // 4 + 2 if b else 1)
                if b == 3:
                    pe.wait_ge(abs_act, 5)
                    pe.wait_ge(abs_dve, 4)
                    nc.tensor.matmul(A[0][:, 0:4], ones32[:], absum[:, 1, 0:4], start=True, stop=True
                                     ).then_inc(total_ready, 1)
                if b == 4:
                    pe.wait_ge(scal, 7)
                if b == 13:
                    pe.wait_ge(tern_p, 4)
                    for c in range(FB):
                        last = nc.tensor.matmul(S[1][:], ones16[:], wp[:, c, :], start=(c == 0),
                                                stop=(c == FB - 1))
                    last.then_inc(tsum_ready, 1)

            def scaled(n, b):
                if b in (6, 9):
                    if b == 6:
                        pe.wait_ge(t_saved, SUB * (n + 1))
                        pe.wait_ge(post_step, POST * (n - 1) + 3)
                    k = 4 * (n - 1) + 2 * (6, 9).index(b)
                    for i in (k, k + 1):
                        pe.wait_ge(u_lo, i + 1)
                        wait(pe, u_saved[i % 2], i // 2)
                        ps = S[i % 2][:].bitcast(F16).rearrange("p (h c t) -> p h c t", h=2, c=DC)
                        for h in range(2):
                            for c in range(DC):
                                last = nc.tensor.transpose(ps[:, h, c, :], ut[:, i % 4, h, c * P:(c + 1) * P],
                                                           id16[:])
                        last.then_inc(u_ready, 1)

            tile(0, False, False, True, first)
            for n in (1, 2):
                tile(n, True, False, True, lambda b, n=n: scaled(n, b))
            with pe.Fori(3, TPB + 1) as n:
                tile(n, True, False, True)
            quad(0, TPB)
            with pe.Fori(TPB + 1, NT - 1) as n:
                tile(n, True, False, True)
            rows(0, NT - 2)
            with pe.Fori(NT - 1, NT + 1) as n:
                tile(n, True, True, True)
            quad(1, NT)
            with pe.Fori(NT + 1, NT + 3) as n:
                tile(n, False, True, True)
            rows(1, NT + 2)
            with pe.Fori(NT + 3, 2 * NT - 1) as n:
                tile(n, False, True, True)
            tile(2 * NT - 1, False, False, False)

        @block.scalar
        def _(act):
            def ln_wait(kind, k, pair, before=None):
                if pair:
                    act.wait_ge(ln_lo[kind], SUB * k + 2)
                else:
                    if kind == "F":
                        act.wait_ge(ln_r["F"], 4 * (k + 1))
                    elif kind == "A":
                        act.wait_ge(ln_r["A"], 2 * (k + 1))
                    if before:
                        act.wait_ge(*before)

            def ln_rows(kind, k, t, dst, pair):
                buf = ub if kind == "Q" else vb
                for s in (2 * pair, 2 * pair + 1):
                    if kind == "F":
                        nb, r = nbF[:, s:s + 1], rf[:, s:s + 1]
                    else:
                        nb, r = nbA[:, bass.ds(SUB * t + s, 1)], rA[:, bass.ds(SUB * t + s, 1)]
                    nc.scalar.activation(buf[:, s % 2, :], X[:, SUB * t + s, :], ACT.Identity, bias=nb, scale=r
                                         ).then_inc(ln_v[kind], 1)
                for s in (2 * pair, 2 * pair + 1):
                    act.wait_ge(ln_v[kind], SUB * k + s + 1)
                    nc.scalar.activation(dst[:, 0, s, :], buf[:, s % 2, :], ACT.Copy).then_inc(ln_hi[kind], 1)

            def save_transposed(i, k, dst, ready, done):
                act.wait_ge(ready, SUB * k + i + 1)
                nc.scalar.activation(dst, QB[i][:].bitcast(F16).rearrange("p (h c t) -> p h c t", h=2, c=DC),
                                     ACT.Copy).then_inc(done, 1)

            def save_q(m, s):
                act.wait_ge(qt_ready, SUB * m + s + 1)
                if s >= 2:
                    act.wait_ge(q_ready, SUB * m + s - 1)
                nc.scalar.activation(qT[:, s % 2], S[s % 2][:].bitcast(F16).rearrange(
                    "p (h c t) -> p h c t", h=2, c=DC), ACT.Copy).then_inc(qt_saved, 1)

            def gelu(n, b):
                B = FB * n + b
                act.wait_ge(h_ready, B + 1)
                wait(act, acc_done, B - RING + 1)
                wait(act, acc_one, (FB - 1) * n + (max(b - RING, 1) if b >= RING else b - RING + 1))
                nc.scalar.activation(gf[:, b % RING, :], H[b % 2][:], ACT.Gelu, scale=hscale[:, 0:1]
                                     ).then_inc(gelu_done, 1)

            def split(n, b, rows):
                B = FB * n + b
                act.wait_ge(gelu_done, B + 1)
                if b >= LAG:
                    act.wait_ge(proj_done, (FB - 1) * n + b - LAG + 1)
                else:
                    wait(act, p_sub, SUB * n)
                nc.scalar.activation(G2[:, b % LAG, 0, :], gf[:, b % RING, :], ACT.Copy, scale=kap[:, 0:1]
                                     ).then_inc(hi_done, 1)
                wait(act, acc_done, B - RING + 1)
                if rows:
                    kind, k, _, _, pair, before = rows
                    ln_wait(kind, k, pair, before)
                nc.scalar.activation(sq[:, b % RING, :], gf[:, b % RING, :], ACT.Square).then_inc(sq_done, 1)

            def tile(n, with_gram, with_q, nxt, hooks=None, next_q=True):
                m = n - (NT - 1)
                t = n + 1 - NT if with_q else n + 1
                for b in range(STEPS + 1):
                    if with_q and b == 0:
                        save_q(m, 0)
                        save_q(m, 1)
                    if b < STEPS:
                        gelu(n, b)
                    rows = []
                    if with_q and next_q and b in (10, 12):
                        rows = ["Q", m + 1, m + 1, hlQ, (b - 10) // 2, (q_saved, SUB * (m + 1))]
                    if with_gram and b in (4, 6):
                        rows = ["A", n - 1, n - 1, hlA, (b - 4) // 2, (ln_lo["F"], SUB * (n + 1))]
                    if nxt and b in (11, 13):
                        rows = ["F", n + 1, t, hl, (b - 11) // 2,
                                (ln_lo["A"], SUB * n) if with_gram else (ln_lo["F"], SUB * (n + 1))]
                    if b:
                        split(n, b - 1, rows)
                    if rows:
                        ln_rows(*rows[:-1])
                    if hooks:
                        hooks(b)
                    if with_q:
                        if b in (6, 7):
                            save_q(m, b - 4)
                act.wait_ge(acc_done, FB * (n + 1) - RING + 1)
                act.wait_ge(acc_one, (FB - 1) * (n + 1))
                nc.scalar.activation(accp[:, 0, 0, :], acc1[:], ACT.Copy, scale=kacc1[:, 0:1]).then_inc(acc_hi, 1)
                act.wait_ge(acc_done, FB * (n + 1))
                nc.scalar.activation(accp[:, 1, 0, :], acc2[:], ACT.Copy, scale=kacc2[:, 0:1]).then_inc(acc_hi, 1)
                if nxt:
                    for i in range(SUB):
                        if i == 0:
                            act.wait_ge(h_ready, FB * (n + 1))
                        save_transposed(i, n + 1, xT[:, :, :, i * P:(i + 1) * P], t_ready, t_saved)

            act.wait_ge(const_ready, 1)
            nc.scalar.activation(warm[:], half[:, 0:1], ACT.Gelu)
            dump = qT[:].rearrange("p a h c t -> p (a h c t)")
            sums_done = [0]

            def abs_sum(src, dst, view=dump):
                wait(act, abs_act, sums_done[0])
                nc.scalar.activation(view, src, ACT.Abs, accum_out=dst).then_inc(abs_act, 1)
                sums_done[0] += 1

            def abs_sum_p(c):
                act.wait_ge(s_wp[c], 16)
                abs_sum(wp_st[c // 2][:, 4 * (c % 2):4 * (c % 2) + 4, :], absum[:, 1, c:c + 1],
                        dump.rearrange("p (c d) -> p c d", d=D))

            act.wait_ge(s_x[0], 16)
            ln_wait("F", 0, 0)
            ln_rows("F", 0, 0, hl, 0)
            act.wait_ge(s_wf[1], 16)
            abs_sum(wf_st[:, 1, :], absum[:, 0, 1:2])
            ln_wait("F", 0, 1)
            ln_rows("F", 0, 0, hl, 1)
            act.wait_ge(s_wf[3], 16)
            abs_sum(wf_st[:, 3, F // 2:F], absum[:, 0, 4:5], dump[:, 0:F // 2])
            for i in range(SUB):
                save_transposed(i, 0, xT[:, :, :, i * P:(i + 1) * P], t_ready, t_saved)
            abs_sum_p(0)
            abs_sum_p(1)
            act.wait_ge(scal, 5)

            def first(b):
                if b == 1:
                    abs_sum_p(2)
                if b == 10:
                    act.wait_ge(s_x[1], 16)

            def scaled(n, b):
                if b in (3, 5):
                    if b == 3:
                        act.wait_ge(u_scale, 1)
                    k = 4 * (n - 1) + b - 3
                    for i in (k, k + 1):
                        wait(act, u_ready, i - 3)
                        nc.scalar.activation(ut[:, i % 4, 0, :], WT_st[:, i, :], ACT.Copy, scale=raS[:, i:i + 1]
                                             ).then_inc(u_hi, 1)
                if b in (5, 8):
                    i = 4 * (n - 1) + 2 * (5, 8).index(b)
                    act.wait_ge(u_ready, i + 1)
                    nc.scalar.activation(U[:, i // 4, :, :, (i % 4) * P:(i % 4 + 1) * P],
                                         S[0][:].bitcast(F16).rearrange("p (h c t) -> p h c t", h=2, c=DC),
                                         ACT.Copy).then_inc(u_saved[0], 1)
                if b == 10:
                    act.wait_ge(s_x[n + 1], 16)

            tile(0, False, False, True, first)
            for n in (1, 2):
                tile(n, True, False, True, lambda b, n=n: scaled(n, b))
            for t in range(4, NT):
                act.wait_ge(s_x[t], 16)
            with act.Fori(3, TPB + 1) as n:
                tile(n, True, False, True)

            def quad(o):
                act.wait_ge(gram_saved, DC * TPB * (o + 1))
                act.wait_ge(acc_lo, 2 * (TPB * (o + 1) + 1))
                act.wait_ge(stat_ready, TPB * (o + 1) + 1)
                for m in range(DC):
                    nc.scalar.activation(GH[:, 0, m, m * P:D], Gacc[:, m, m * P:D], ACT.Copy).then_inc(g_hi, 1)
                act.wait_ge(gt_ready, 2 * o + 1)
                k = 0
                for i in range(DC - 1):
                    w = DC - 1 - i
                    last = nc.scalar.activation(
                        GH[:, 0, i + 1:DC, i * P:(i + 1) * P],
                        S[0][:].bitcast(F16)[:, k * P:(k + w) * P].rearrange("p (c d) -> p c d", c=w), ACT.Copy)
                    k += w
                last.then_inc(gt_saved, 1)
                for g in range(DC):
                    m = DC - 1 - g
                    if g == 0:
                        act.wait_ge(mu_saved, TPB * (o + 1))
                        act.wait_ge(ln_lo["F"], SUB * (TPB * (o + 1) + 2))
                    act.wait_ge(s_wst[g % 2], 16 * (2 * o + g // 2 + 1))
                    for i, j in enumerate((1, 2, 0)):
                        if g > 1:
                            act.wait_ge(mw_ready, 3 * ((DC - 1) * o + g - 2) + i + 1)
                        nc.scalar.activation((mu_sum if g == 0 else mu_term)[i], Wst[g % 2][:, j, :], ACT.Copy,
                                             scale=mu[:, m:m + 1]).then_inc(mw_prod, 1)

            quad(0)
            with act.Fori(TPB + 1, NT - 1) as n:
                tile(n, True, False, True)
            for j in range(2):
                ln_wait("Q", 0, j)
                ln_rows("Q", 0, 0, hlQ, j)
            with act.Fori(NT - 1, NT + 1) as n:
                tile(n, True, True, True)
            quad(1)
            with act.Fori(NT + 1, NT + 3) as n:
                tile(n, False, True, True)
            with act.Fori(NT + 3, 2 * NT - 2) as n:
                tile(n, False, True, True)
            tile(2 * NT - 2, False, True, True, next_q=False)
            tile(2 * NT - 1, False, False, False)

        @block.vector
        def _(dve):
            V = nc.vector

            def ln_stats(kind, k, s, row):
                V.bn_stats((st if kind == "F" else stA)[:, s, :], X[:, row, :]).then_inc(ln_stat[kind], 1)

            def ln_var(kind, k, t):
                stats = st if kind == "F" else stA
                A0 = 5 * k
                dve.wait_ge(ln_stat[kind], SUB * (k + 1))
                V.tensor_tensor(msum[:], stats[:, :, 1], stats[:, :, 4], ALU.add).then_inc(ln_aggr[kind], 1)
                V.tensor_tensor(mdif[:], stats[:, :, 1], stats[:, :, 4], ALU.subtract).then_inc(ln_aggr[kind], 1)
                V.tensor_tensor(vsum[:], stats[:, :, 2], stats[:, :, 5], ALU.add).then_inc(ln_aggr[kind], 1)
                dve.wait_ge(ln_aggr[kind], A0 + 2)
                V.scalar_tensor_tensor(vdif[:], mdif[:], D / 4.0, mdif[:], ALU.mult, ALU.mult
                                       ).then_inc(ln_aggr[kind], 1)
                mean = mF[:] if kind == "F" else mA[:]
                V.tensor_scalar(mean, msum[:], 0.5, None, ALU.mult).then_inc(ln_mean[kind], 1)
                dve.wait_ge(ln_aggr[kind], A0 + 4)
                V.tensor_tensor(vtot[:], vsum[:], vdif[:], ALU.add).then_inc(ln_aggr[kind], 1)
                dve.wait_ge(ln_aggr[kind], A0 + 5)
                if kind == "A":
                    V.tensor_scalar(veA[:], vtot[:], 1.0 / D, EPS_LN, ALU.mult, ALU.add).then_inc(ln_pre["A"], 1)
                else:
                    V.tensor_scalar(ve[:], vtot[:], (1.0 + EPS_BIT) / D, EPS_LN * EPS_BIT, ALU.mult, ALU.add
                                    ).then_inc(ln_pre["F"], 1)
                    V.reciprocal(rz[:], vtot[:]).then_inc(ln_r["F"], 1)

            def ln_scale(kind, k, t):
                if kind == "A":
                    dve.wait_ge(ln_pow["A"], k + 1)
                    V.tensor_scalar(rA[:, bass.ts(t, SUB)], pwA[:], XS, None, ALU.mult).then_inc(ln_r["A"], 1)
                    dve.wait_ge(ln_r["A"], 2 * k + 1)
                    dve.wait_ge(ln_mean["A"], k + 1)
                    V.scalar_tensor_tensor(nbA[:, bass.ts(t, SUB)], mA[:], -1.0, rA[:, bass.ts(t, SUB)],
                                           ALU.mult, ALU.mult).then_inc(ln_r["A"], 1)
                else:
                    dve.wait_ge(ln_r["F"], 4 * k + 1)
                    V.tensor_tensor(zz[:], rz[:], vtot[:], ALU.mult).then_inc(ln_r["F"], 1)
                    dve.wait_ge(ln_r["F"], 4 * k + 2)
                    dve.wait_ge(ln_pow["F"], k + 1)
                    V.scalar_tensor_tensor(rf[:], pw[:], XS, zz[:], ALU.mult, ALU.mult).then_inc(ln_r["F"], 1)
                    dve.wait_ge(ln_r["F"], 4 * k + 3)
                    dve.wait_ge(ln_mean["F"], k + 1)
                    V.scalar_tensor_tensor(nbF[:], mF[:], -1.0, rf[:], ALU.mult, ALU.mult).then_inc(ln_r["F"], 1)

            def ln_low(kind, k, s, dst):
                buf = ub if kind == "Q" else vb
                dve.wait_ge(ln_hi[kind], SUB * k + s + 1)
                dve.wait_ge(ln_v[kind], SUB * k + s + 1)
                V.tensor_tensor(dst[:, 1, s, :], buf[:, s % 2, :], dst[:, 0, s, :], ALU.subtract
                                ).then_inc(ln_lo[kind], 1)

            def ln_lows(kind, k, pair, dst):
                ln_low(kind, k, 2 * pair, dst)
                ln_low(kind, k, 2 * pair + 1, dst)

            def hidden(n, b):
                B = FB * n + b
                dve.wait_ge(hi_done, B + 1)
                V.scalar_tensor_tensor(G2[:, b % LAG, 1, :], gf[:, b % RING, :], kap[:, 0:1], G2[:, b % LAG, 0, :],
                                       ALU.mult, ALU.subtract).then_inc(lo_done, 1)
                dve.wait_ge(sq_done, B + 1)
                if b == 0:
                    V.tensor_copy(acc2[:], sq[:, 0, :]).then_inc(acc_done, 1)
                else:
                    dve.wait_ge(acc_done, B)
                    V.tensor_tensor(acc2[:], acc2[:], sq[:, b % RING, :], ALU.add).then_inc(acc_done, 1)

            def post_scalars(n):
                for j, (a, k) in enumerate(((acc1, kacc1), (acc2, kacc2))):
                    dve.wait_ge(acc_hi, 2 * n + j + 1)
                    V.scalar_tensor_tensor(accp[:, j, 1, :], a[:], k[:, 0:1], accp[:, j, 0, :],
                                           ALU.mult, ALU.subtract).then_inc(acc_lo, 1)
                P0 = POST * n
                dve.wait_ge(stat_ready, n + 1)
                V.tensor_scalar(negmk[:], S[0][:, 0:SUB], -1.0 / (AS1 * F), None, ALU.mult).then_inc(post_step, 1)
                dve.wait_ge(post_step, P0 + 1)
                V.tensor_tensor(m2[:], negmk[:], negmk[:], ALU.mult).then_inc(post_step, 1)
                dve.wait_ge(post_step, P0 + 2)
                V.scalar_tensor_tensor(var[:], S[0][:, SUB:2 * SUB], 1.0 / (AS2 * F), m2[:], ALU.mult, ALU.subtract
                                       ).then_inc(post_step, 1)
                dve.wait_ge(post_step, P0 + 3)
                V.tensor_scalar(varc[:], var[:], 0.0, None, ALU.max).then_inc(post_step, 1)
                dve.wait_ge(post_step, P0 + 4)
                V.tensor_scalar(veP[:], varc[:], ksq[:, 0:1], EPS_BIT, ALU.mult, ALU.add).then_inc(post_pre, 1)
                V.reciprocal(rzP[:], varc[:]).then_inc(post_step, 1)
                dve.wait_ge(post_step, P0 + 5)
                V.tensor_tensor(zP[:], rzP[:], varc[:], ALU.mult).then_inc(post_step, 1)

            def post_rows(n, t):
                dve.wait_ge(post_step, POST * n + 6)
                dve.wait_ge(post_pow, n + 1)
                V.scalar_tensor_tensor(cP[:], pwP[:], cs[:, 0:1], zP[:], ALU.mult, ALU.mult
                                       ).then_inc(post_step, 1)
                dve.wait_ge(post_step, POST * n + 7)
                V.tensor_tensor(nmc[:], negmk[:], cP[:], ALU.mult).then_inc(post_step, 1)
                dve.wait_ge(post_step, POST * (n + 1))
                for s in range(SUB):
                    row = SUB * t + s
                    V.scalar_tensor_tensor(X[:, row, :], Tsum[:], nmc[:, s:s + 1], X[:, row, :],
                                           ALU.mult, ALU.add).then_inc(x_pre, 1)
                post_product(n, t, 0)

            def post_product(n, t, pair):
                for s in (2 * pair, 2 * pair + 1):
                    row = SUB * t + s
                    dve.wait_ge(x_pre, SUB * n + s + 1)
                    dve.wait_ge(p_sub, SUB * n + s + 1)
                    V.scalar_tensor_tensor(X[:, row, :], A[s][:], cP[:, s:s + 1], X[:, row, :],
                                           ALU.mult, ALU.add).then_inc(x_sub, 1)

            def gram_add(n, m):
                dve.wait_ge(gram_ready, DC * (n - 1) + m + 1)
                w = D - m * P
                if m == DC - 1:
                    V.scalar_tensor_tensor(mu[:], S[m % 2][:, 256:256 + DC], TS / XS, mu[:],
                                           ALU.mult, ALU.add).then_inc(mu_saved, 1)
                V.scalar_tensor_tensor(Gacc[:, m, m * P:D], S[m % 2][:, 0:w], GS / XS / XS, Gacc[:, m, m * P:D],
                                       ALU.mult, ALU.add).then_inc(gram_saved, 1)

            def q_add_rows(n, s):
                m = n - (NT - 1)
                row = SUB * m + s
                k = SUB * m + s
                dve.wait_ge(q_ready, k + 1)
                if s >= 2:
                    dve.wait_ge(q_saved, k - 1)
                V.tensor_tensor(ub[:, s % 2, :], S[s % 2][:], Srow, ALU.mult).then_inc(q_mul, 1)
                V.tensor_tensor(X[:, row, :], X[:, row, :], Brow, ALU.add).then_inc(q_add, 1)
                dve.wait_ge(q_mul, k + 1)
                dve.wait_ge(q_add, k + 1)
                V.tensor_tensor(X[:, row, :], X[:, row, :], ub[:, s % 2, :], ALU.add).then_inc(q_saved, 1)

            def tile(n, with_gram, with_q, nxt, hooks=None, next_q=True, post=True):
                m = n - (NT - 1)
                t = n + 1 - NT if with_q else n + 1
                t_last = n - 1 if with_gram else n - 1 - NT
                if post:
                    post_rows(n - 1, t_last)
                for b in range(STEPS):
                    if with_gram and b < 2:
                        dve.wait_ge(x_sub, SUB * (n - 1) + 2 * (b + 1))
                    if with_q and b in (5, 9):
                        dve.wait_ge(q_saved, SUB * m + (2 if b == 5 else 4))
                    if nxt and b == 10:
                        ln_scale("F", n + 1, t)
                    hidden(n, b)
                    if post and b == 0:
                        post_product(n - 1, t_last, 1)
                    if hooks:
                        hooks(b)
                    if with_q:
                        if next_q and b in (10, 12):
                            ln_lows("Q", m + 1, (b - 10) // 2, hlQ)
                        if b in (2, 3, 7, 8):
                            q_add_rows(n, (2, 3, 7, 8).index(b))
                    if with_gram:
                        if b < 2:
                            for s in (2 * b, 2 * b + 1):
                                ln_stats("A", n - 1, s, SUB * (n - 1) + s)
                        if b == 1:
                            ln_var("A", n - 1, n - 1)
                        if b == 2:
                            ln_scale("A", n - 1, n - 1)
                        if b in (4, 6):
                            ln_lows("A", n - 1, (b - 4) // 2, hlA)
                        if 10 <= b < 14:
                            gram_add(n, b - 10)
                    if nxt:
                        s01, s23 = (5, 9) if with_q else (7, 8)
                        if b in (s01, s23):
                            for s in ((0, 1) if b == s01 else (2, 3)):
                                ln_stats("F", n + 1, s, SUB * t + s)
                        if b == s23:
                            ln_var("F", n + 1, t)
                        if b in (11, 13):
                            ln_lows("F", n + 1, (b - 11) // 2, hl)
                post_scalars(n)

            def ternary(j, src, dst, low, done):
                if pieces:
                    dve.wait_ge(*pieces[-1])
                V.tensor_scalar(low, src, theta[:, j, 1:2], None, ALU.is_lt).then_inc(low_ready, 1)
                dve.wait_ge(low_ready, len(pieces) + 1)
                V.scalar_tensor_tensor(dst, src, theta[:, j, 0:1], low, ALU.is_gt, ALU.subtract
                                       ).then_inc(done, 1)
                pieces.append((done, sum(d is done for d, _ in pieces) + 1))

            pieces = []

            def ternary_f(a, w):
                ternary(0, wf_st[:, :, a:a + w], wf[:, :, a:a + w], low16[:, :, 0:w], tern_f)

            def ternary_p(i):
                ternary(1, wp_st[i // 2][:, 4 * (i % 2):4 * (i % 2) + 4, :], wp[:, 4 * i:4 * i + 4, :], low16, tern_p)

            def abs_sum(c, a, w, k):
                dve.wait_ge(s_wf[c], 16)
                V.tensor_reduce(absum[:, 0, k:k + 1], wf_st[:, c, a:a + w], AX.X, ALU.add,
                                apply_absolute_value=True).then_inc(abs_dve, 1)

            dve.wait_ge(s_x[0], 16)
            for s in range(SUB):
                ln_stats("F", 0, s, s)
            ln_var("F", 0, 0)
            abs_sum(0, 0, F, 0)
            ln_scale("F", 0, 0)
            V.memset(Gacc[:], 0.0).then_inc(g_zero, 1)
            V.memset(mu[:], 0.0).then_inc(g_zero, 1)
            ln_lows("F", 0, 0, hl)
            abs_sum(2, 0, F, 2)
            ln_lows("F", 0, 1, hl)
            abs_sum(3, 0, F // 2, 3)
            dve.wait_ge(total_ready, 1)
            V.tensor_reduce(gam[:, 0:1], A[1][:, 0:5], AX.X, ALU.add).then_inc(scal, 1)
            dve.wait_ge(scal, 1)
            V.tensor_scalar(gam[:, 0:1], gam[:, 0:1], 1.0 / (D * F), None, ALU.mult).then_inc(scal, 1)
            dve.wait_ge(scal, 2)
            V.tensor_scalar(theta[:, 0, 0:1], gam[:, 0:1], EPS_BIT, 0.5, ALU.add, ALU.mult).then_inc(thr_f, 1)
            V.tensor_scalar(theta[:, 0, 1:2], gam[:, 0:1], EPS_BIT, -0.5, ALU.add, ALU.mult).then_inc(thr_f, 1)
            V.tensor_scalar(hscale[:], gam[:, 0:1], 1.0 / XS, None, ALU.mult).then_inc(scal, 1)
            V.tensor_scalar(kinv[:], gam[:, 0:1], 1.0 / 64, None, ALU.mult).then_inc(scal, 1)
            dve.wait_ge(scal, 4)
            V.reciprocal(kap[:], kinv[:]).then_inc(scal, 1)
            V.tensor_scalar(cs[:], gam[:, 0:1], 0.5 / 64, None, ALU.mult).then_inc(scal, 1)
            V.tensor_tensor(ksq[:], kinv[:], kinv[:], ALU.mult).then_inc(k_ready, 1)
            dve.wait_ge(scal, 5)
            V.tensor_scalar(kacc1[:], kap[:], AS1, None, ALU.mult).then_inc(k_ready, 1)
            V.scalar_tensor_tensor(kacc2[:], kap[:], AS2, kap[:], ALU.mult, ALU.mult).then_inc(k_ready, 1)
            dve.wait_ge(k_ready, 3)
            dve.wait_ge(thr_f, 2)
            ternary_f(0, P)
            ternary_f(P, 3 * P)
            ternary_f(4 * P, 4 * P)

            def first(b):
                if b == 0:
                    dve.wait_ge(s_wp[3], 16)
                    V.tensor_reduce(absum[:, 1, 3:4], wp_st[1][:, 4:8, :], AX.XY, ALU.add,
                                    apply_absolute_value=True).then_inc(abs_dve, 1)
                if b == 1:
                    dve.wait_ge(total_ready, 2)
                    V.tensor_reduce(gam[:, 1:2], A[0][:, 0:4], AX.X, ALU.add).then_inc(scal, 1)
                    dve.wait_ge(scal, 7)
                    V.tensor_scalar(gam[:, 1:2], gam[:, 1:2], 1.0 / (D * F), None, ALU.mult).then_inc(scal, 1)
                    dve.wait_ge(scal, 8)
                    V.tensor_scalar(theta[:, 1, 0:1], gam[:, 1:2], EPS_BIT, 0.5, ALU.add, ALU.mult
                                    ).then_inc(thr_p, 1)
                    V.tensor_scalar(theta[:, 1, 1:2], gam[:, 1:2], EPS_BIT, -0.5, ALU.add, ALU.mult
                                    ).then_inc(thr_p, 1)
                    V.tensor_tensor(cs[:], cs[:], gam[:, 1:2], ALU.mult).then_inc(thr_p, 1)
                    dve.wait_ge(thr_p, 3)
                if b in (1, 3, 7, 9):
                    ternary_p((1, 3, 7, 9).index(b))
                if b in (2, 5):
                    ternary_f(8 * P if b == 2 else 12 * P, 4 * P)
                if b == 6:
                    dve.wait_ge(s_x[1], 16)
                if b == 13:
                    dve.wait_ge(tsum_ready, 1)
                    V.tensor_copy(Tsum[:], S[1][:]).then_inc(tsum_saved, 1)
                if b in (10, 12):
                    dve.wait_ge(s_WT, 16)
                    r = slice(0, 4) if b == 10 else slice(4, 8)
                    V.tensor_reduce(acol[:, r], WT_st[:, r, :], AX.X, ALU.max, apply_absolute_value=True
                                    ).then_inc(u_chain, 1)

            def scaled(n, b):
                if n == 1 and b == 0:
                    dve.wait_ge(s_b, 16)
                    V.tensor_reduce(babs[:], bcol[:, 0:8].rearrange("p (c a) -> p c a", a=1), AX.X, ALU.max,
                                    apply_absolute_value=True).then_inc(u_chain, 1)
                    dve.wait_ge(u_chain, 3)
                    V.tensor_tensor(acol[:], acol[:], babs[:], ALU.max).then_inc(u_chain, 1)
                    dve.wait_ge(u_chain, 4)
                    V.reciprocal(ra[:], acol[:]).then_inc(u_chain, 1)
                    dve.wait_ge(u_chain, 5)
                    V.tensor_scalar(raS[:], ra[:], US, None, ALU.mult).then_inc(u_scale, 1)
                    V.tensor_tensor(bn[:], bcol[:, 0:8], ra[:], ALU.mult).then_inc(u_chain, 1)
                if b in (3, 5):
                    k = 4 * (n - 1) + b - 3
                    for i in (k, k + 1):
                        dve.wait_ge(u_hi, i + 1)
                        V.scalar_tensor_tensor(ut[:, i % 4, 1, :], WT_st[:, i, :], raS[:, i:i + 1],
                                               ut[:, i % 4, 0, :], ALU.mult, ALU.subtract).then_inc(u_lo, 1)
                if b in (5, 8):
                    i = 4 * (n - 1) + 2 * (5, 8).index(b) + 1
                    dve.wait_ge(u_ready, i + 1)
                    V.tensor_copy(U[:, i // 4, :, :, (i % 4) * P:(i % 4 + 1) * P],
                                  S[1][:].bitcast(F16).rearrange("p (h c t) -> p h c t", h=2, c=DC)
                                  ).then_inc(u_saved[1], 1)
                if b == 6:
                    dve.wait_ge(s_x[n + 1], 16)

            tile(0, False, False, True, first, post=False)
            dve.wait_ge(g_zero, 2)
            dve.wait_ge(tsum_saved, 1)
            for n in (1, 2):
                tile(n, True, False, True, lambda b, n=n: scaled(n, b))
            for t in range(4, NT):
                dve.wait_ge(s_x[t], 16)
            with dve.Fori(3, TPB + 1) as n:
                tile(n, True, False, True)

            def quad(o, n):
                dve.wait_ge(gram_saved, DC * TPB * (o + 1))
                for m in range(DC):
                    dve.wait_ge(g_hi, DC * o + m + 1)
                    V.tensor_tensor(GH[:, 1, m, m * P:D], Gacc[:, m, m * P:D], GH[:, 0, m, m * P:D],
                                    ALU.subtract).then_inc(g_lo, 1)
                dve.wait_ge(gt_ready, 2 * (o + 1))
                k = 0
                for i in range(DC - 1):
                    w = DC - 1 - i
                    last = V.tensor_copy(GH[:, 1, i + 1:DC, i * P:(i + 1) * P],
                                         S[1][:].bitcast(F16)[:, k * P:(k + w) * P].rearrange("p (c d) -> p c d", c=w))
                    k += w
                last.then_inc(gt_saved, 1)
                post_rows(n, n % NT)
                post_product(n, n % NT, 1)
                for g in range(DC):
                    m = DC - 1 - g
                    r = 2 if g % 2 == 0 else 0
                    dve.wait_ge(s_wst[g % 2], 16 * (2 * o + g // 2 + 1))
                    wq_, wk_, wv_ = (Wst[g % 2][:, j, :] for j in range(3))
                    dve.wait_ge(gu_ready, 2 * (DC * o + g) + 1)
                    if g == 0:
                        V.tensor_tensor(sums[:, 0, :], QB[r][:], wk_, ALU.mult).then_inc(qd, 1)
                        V.tensor_tensor(sums[:, 1, :], QB[r][:], wv_, ALU.mult).then_inc(gu_saved, 1)
                        dve.wait_ge(gu_ready, 2 * (DC * o + g) + 2)
                        V.tensor_tensor(sums[:, 2, :], QB[r + 1][:], wq_, ALU.mult).then_inc(gu_saved, 1)
                    else:
                        dve.wait_ge(qd, QN * o + 3 * g - 2)
                        V.tensor_tensor(term[0], QB[r][:], wk_, ALU.mult).then_inc(qt, 1)
                        V.tensor_tensor(term[1], QB[r][:], wv_, ALU.mult).then_inc(gu_saved, 1)
                        dve.wait_ge(qt, (DC - 1) * o + g)
                        V.tensor_tensor(sums[:, 0, :], sums[:, 0, :], term[0], ALU.add).then_inc(qd, 1)
                        dve.wait_ge(gu_ready, 2 * (DC * o + g) + 2)
                        V.tensor_tensor(term[2], QB[r + 1][:], wq_, ALU.mult).then_inc(gu_saved, 1)
                        dve.wait_ge(gu_saved, 2 * (DC * o + g) + 1)
                        V.tensor_tensor(sums[:, 1, :], sums[:, 1, :], term[1], ALU.add).then_inc(qd, 1)
                        dve.wait_ge(gu_saved, 2 * (DC * o + g) + 2)
                        V.tensor_tensor(sums[:, 2, :], sums[:, 2, :], term[2], ALU.add).then_inc(qd, 1)
                dve.wait_ge(mw_ready, 3 * (DC - 1) * (o + 1))
                V.memset(mu[:], 0.0).then_inc(g_zero, 1)
                V.memset(Gacc[:], 0.0).then_inc(g_zero, 1)
                dve.wait_ge(g_zero, 2 * (o + 2))
                dve.wait_ge(red_ready, o + 1)
                V.tensor_copy(red[:], H[0][:, 0:6 * DC]).then_inc(red_saved, 1)

            def quad_scale(o):
                def chain(ins):
                    c0[0] += 1
                    ins.then_inc(red_chain, 1)
                    dve.wait_ge(red_chain, c0[0])

                def chain_v(ins):
                    c1[0] += 1
                    ins.then_inc(sc_chain, 1)
                    dve.wait_ge(sc_chain, c1[0])

                c0, c1 = [RC * o], [5 * o]
                dve.wait_ge(red_saved, o + 1)
                kk_, kv_, qq_, mk, mv, mq = (red[:, DC * i:DC * (i + 1)] for i in range(6))
                bq, bk, bv = (bcol[:, DC * i:DC * (i + 1)] for i in range(3))
                n_q, n_k = bn[:, 0:DC], bn[:, DC:2 * DC]
                r_q, r_k = ra[:, 0:DC], ra[:, DC:2 * DC]
                chain(V.tensor_tensor(mk, mk, r_k, ALU.mult))
                chain(V.scalar_tensor_tensor(k1[:], n_k, float(T * TS), mk, ALU.mult, ALU.add))
                chain(V.tensor_tensor(mq, mq, r_q, ALU.mult))
                chain(V.scalar_tensor_tensor(q1[:], n_q, float(T * TS), mq, ALU.mult, ALU.add))
                chain(V.tensor_tensor(kk[:], bk, mk, ALU.mult))
                chain(V.tensor_tensor(kk[:], kk[:], kk_, ALU.add))
                chain(V.tensor_tensor(qq[:], bq, mq, ALU.mult))
                chain(V.tensor_tensor(qq[:], qq[:], qq_, ALU.add))
                chain(V.tensor_tensor(k2[:], bk, k1[:], ALU.mult))
                chain(V.tensor_tensor(kk[:], kk[:], k2[:], ALU.add))
                chain(V.tensor_tensor(q2[:], bq, q1[:], ALU.mult))
                chain(V.tensor_tensor(qq[:], qq[:], q2[:], ALU.add))
                chain(V.tensor_tensor(kk[:], kk[:], r_k, ALU.mult))
                chain(V.tensor_tensor(qq[:], qq[:], r_q, ALU.mult))
                chain(V.tensor_tensor(prod[:], kk[:], qq[:], ALU.mult))
                chain_v(V.tensor_tensor(kv[:], bv, k1[:], ALU.mult))
                chain_v(V.tensor_tensor(kv[:], kv[:], kv_, ALU.add))
                chain_v(V.tensor_tensor(k2[:], n_k, mv, ALU.mult))
                chain_v(V.tensor_tensor(kv[:], kv[:], k2[:], ALU.add))
                dve.wait_ge(s_pow, o + 1)
                chain_v(V.tensor_tensor(sc2[:], kv[:], ip[:], ALU.mult))
                V.tensor_scalar(scol[:], sc2[:], 1.0 / (XS * US), None, ALU.mult).then_inc(sc_one, 1)
                V.tensor_tensor(bsc[:], sc2[:], n_q, ALU.mult).then_inc(sc_one, 1)
                dve.wait_ge(sc_one, 2 * (o + 1))
                for j, col in ((0, scol), (1, bsc)):
                    for c in range(DC):
                        last = V.tensor_scalar(diag[:, j, c, :], id32[:], col[:, c:c + 1], None, ALU.mult)
                    last.then_inc(s_diag, 1)

            def quad_rows(o):
                for j, row in ((0, Srow), (1, Brow)):
                    dve.wait_ge(s_row, 2 * o + j + 1)
                    V.tensor_copy(row, S[j][:]).then_inc(s_saved, 1)
                dve.wait_ge(s_saved, 2 * (o + 1))

            quad(0, TPB)
            quad_scale(0)
            tile(TPB + 1, True, False, True, post=False)
            for n in range(TPB + 2, NT - 1):
                tile(n, True, False, True)
            ln_lows("Q", 0, 0, hlQ)
            quad_rows(0)
            ln_lows("Q", 0, 1, hlQ)
            with dve.Fori(NT - 1, NT + 1) as n:
                tile(n, True, True, True)
            quad(1, NT)
            quad_scale(1)
            tile(NT + 1, False, True, True, post=False)
            tile(NT + 2, False, True, True)
            quad_rows(1)
            with dve.Fori(NT + 3, 2 * NT - 2) as n:
                tile(n, False, True, True)
            tile(2 * NT - 2, False, True, True, next_q=False)
            tile(2 * NT - 1, False, False, False)
            post_rows(2 * NT - 1, NT - 1)
            post_product(2 * NT - 1, NT - 1, 1)


def kernel(L0_attn_x, L0_attn_W, L0_attn_b, L0_ffn_w_fc, L0_ffn_w_proj):
    import numpy as np
    import concourse.bacc as bacc
    from concourse.bass_utils import run_bass_kernel_spmd as run

    nc = bacc.Bacc("TRN2", target_bir_lowering=False, num_devices=1)
    arrays = {
        "x": np.ascontiguousarray(L0_attn_x),
        "WT": np.ascontiguousarray(np.transpose(L0_attn_W)),
        "W": np.ascontiguousarray(L0_attn_W),
        "b": np.ascontiguousarray(L0_attn_b),
        "wfT": np.ascontiguousarray(np.transpose(L0_ffn_w_fc)),
        "wpT": np.ascontiguousarray(np.transpose(L0_ffn_w_proj)),
    }
    args = [nc.dram_tensor(n, a.shape, F32, kind="ExternalInput").ap() for n, a in arrays.items()]
    out = nc.dram_tensor("out", arrays["x"].shape, F32, kind="ExternalOutput").ap()
    macaron_kernel(nc, *args, out)
    return run(nc, [arrays], core_ids=[0]).results[0]["out"]
```
